# Optimizing a Trainium2 kernel written in Bass

```python
import numpy as np
import jax
import jax.numpy as jnp

def _softmax(x, axis=-1):
    return jax.nn.softmax(x, axis=axis)

def _gelu(x):
    return jax.nn.gelu(x, approximate=True)

def _silu(x):
    return jax.nn.silu(x)

def _sigmoid(x):
    return jax.nn.sigmoid(x)

def _layernorm(x, axis=-1, eps=1e-05):
    m = jnp.mean(x, axis=axis, keepdims=True)
    v = jnp.var(x, axis=axis, keepdims=True)
    return (x - m) / jnp.sqrt(v + eps)

def _scatter_add(tgt, idx, src, axis=0):
    return tgt.at[idx].add(src)

def _segment_sum(src, seg, n):
    return jax.ops.segment_sum(src, seg, n)
kernel_name = 'mk_audio_tower_d2_tok_audfeat512_r4_5506f5'

def setup_inputs(seed: int=0):
    np.random.seed(seed)
    _w = jnp.asarray

    def _rec_inputs():
        import jax
        import jax.numpy as jnp
        _rk = jax.random.key(seed)
        x = 7.22013e-05 + 1.00017 * jax.random.normal(jax.random.fold_in(_rk, 1), (64, 375, 128), jnp.float32)
        return x
    x = _rec_inputs()

    def _L0_tok_setup():
        import jax, jax.numpy as jnp
        import numpy as np
        D_MODEL = 128
        N_HEADS = 4
        EPS = 1e-05

        def _layernorm(x, g, b):
            m = jnp.mean(x, axis=-1, keepdims=True)
            v = jnp.mean((x - m) ** 2, axis=-1, keepdims=True)
            return (x - m) * jax.lax.rsqrt(v + EPS) * g + b
        key = jax.random.key(seed)
        ks = jax.random.split(key, 12)
        B, S, d, H = (4, 1024, D_MODEL, N_HEADS)
        s = 1.0 / np.sqrt(d)
        inp = {'X': jax.random.normal(ks[0], (B, S, d), dtype=jnp.float32), 'rseq': 128, 'g1': jnp.ones((d,), jnp.float32), 'b1': jnp.zeros((d,), jnp.float32), 'Wq': jax.random.normal(ks[1], (H, d, d), jnp.float32) * s, 'bq': jnp.zeros((H, d), jnp.float32), 'Wk': jax.random.normal(ks[2], (H, d, d), jnp.float32) * s, 'bk': jnp.zeros((H, d), jnp.float32), 'Wv': jax.random.normal(ks[3], (H, d, d), jnp.float32) * s, 'bv': jnp.zeros((H, d), jnp.float32), 'Wo': jax.random.normal(ks[4], (H * d, d), jnp.float32) / np.sqrt(H * d), 'bo': jnp.zeros((d,), jnp.float32), 'g2': jnp.ones((d,), jnp.float32), 'b2': jnp.zeros((d,), jnp.float32), 'Wf': jax.random.normal(ks[5], (d, d), jnp.float32) * s, 'bf': jnp.zeros((d,), jnp.float32)}
        return inp
    _L0_tok_all = _L0_tok_setup()
    _L0_tok_in = {k: v for k, v in _L0_tok_all.items() if k in ('g1', 'b1', 'Wq', 'bq', 'Wk', 'bk', 'Wv', 'bv', 'Wo', 'bo', 'g2', 'b2', 'Wf', 'bf')}
    del _L0_tok_all

    def _L0_attn_setup():
        import math
        import jax, jax.numpy as jnp
        import numpy as np
        FACTOR = 1
        key = jax.random.key(seed)
        k1, k2 = jax.random.split(key, 2)
        B, T, D = (8, 1024, 128)
        x = jax.random.normal(k1, (B, T, D), dtype=jnp.float32)
        W = jax.random.normal(k2, (D, D), dtype=jnp.float32) / math.sqrt(D)
        b = jnp.zeros((D,), dtype=jnp.float32)
        return {'x': x, 'W': W, 'b': b}
    _L0_attn_all = _L0_attn_setup()
    _L0_attn_in = {k: v for k, v in _L0_attn_all.items() if k in ('W', 'b')}
    del _L0_attn_all

    def _L0_ffn_setup():
        import jax, jax.numpy as jnp
        import numpy as np
        B, C, IN_LEN, OUT_LEN, E, TOP_K, N_I = (1, 2048, 128, 128, 8, 2, 16)
        key = jax.random.key(seed)
        ks = jax.random.split(key, 8)
        w = lambda k, shape, sc=0.02: jax.random.normal(k, shape, dtype=jnp.float32) * sc
        return {'x': jax.random.normal(ks[0], (B, C, IN_LEN), dtype=jnp.float32), 'Ins_tk': jax.random.normal(ks[1], (B, N_I, OUT_LEN), dtype=jnp.float32), 'gate_w': w(ks[2], (IN_LEN, E)), 'expert_w': w(ks[3], (E, IN_LEN, OUT_LEN)), 'expert_b': jnp.zeros((E, OUT_LEN), dtype=jnp.float32), 'gamma_w': w(ks[4], (E, OUT_LEN)), 'beta_w': w(ks[5], (E, OUT_LEN, OUT_LEN)), 'rmod_w': w(ks[6], (OUT_LEN, E))}
    _L0_ffn_all = _L0_ffn_setup()
    _L0_ffn_in = {k: v for k, v in _L0_ffn_all.items() if k in ('Ins_tk', 'gate_w', 'expert_w', 'expert_b', 'gamma_w', 'beta_w', 'rmod_w')}
    del _L0_ffn_all

    def _L1_attn_setup():
        import jax, jax.numpy as jnp
        import numpy as np
        key = jax.random.key(seed)
        x = jax.random.normal(key, (8, 512, 128), dtype=jnp.float32)
        return {'x': x}
    _L1_attn_all = _L1_attn_setup()
    _L1_attn_in = {k: v for k, v in _L1_attn_all.items() if k in ()}
    del _L1_attn_all

    def _L1_ffn_setup():
        import jax, jax.numpy as jnp
        import numpy as np
        B, L, H, E, F, C = (8, 2048, 128, 8, 256, 2)
        key = jax.random.key(seed)
        ks = jax.random.split(key, 4)
        x = jax.random.normal(ks[0], (B, L, H), jnp.float32)
        Wg = jax.random.normal(ks[1], (H, E), jnp.float32) * H ** (-0.5)
        W1 = jax.random.normal(ks[2], (E, H, F), jnp.float32) * H ** (-0.5)
        b1 = jnp.zeros((E, F), jnp.float32)
        W2 = jax.random.normal(ks[3], (E, F, H), jnp.float32) * F ** (-0.5)
        b2 = jnp.zeros((E, H), jnp.float32)
        return {'x': x, 'Wg': Wg, 'W1': W1, 'b1': b1, 'W2': W2, 'b2': b2}
    _L1_ffn_all = _L1_ffn_setup()
    _L1_ffn_in = {k: v for k, v in _L1_ffn_all.items() if k in ('Wg', 'W1', 'b1', 'W2', 'b2')}
    del _L1_ffn_all
    return {'x': x, 'L0_tok_g1': _L0_tok_in['g1'], 'L0_tok_b1': _L0_tok_in['b1'], 'L0_tok_Wq': _L0_tok_in['Wq'], 'L0_tok_bq': _L0_tok_in['bq'], 'L0_tok_Wk': _L0_tok_in['Wk'], 'L0_tok_bk': _L0_tok_in['bk'], 'L0_tok_Wv': _L0_tok_in['Wv'], 'L0_tok_bv': _L0_tok_in['bv'], 'L0_tok_Wo': _L0_tok_in['Wo'], 'L0_tok_bo': _L0_tok_in['bo'], 'L0_tok_g2': _L0_tok_in['g2'], 'L0_tok_b2': _L0_tok_in['b2'], 'L0_tok_Wf': _L0_tok_in['Wf'], 'L0_tok_bf': _L0_tok_in['bf'], 'L0_attn_W': _L0_attn_in['W'], 'L0_attn_b': _L0_attn_in['b'], 'L0_ffn_Ins_tk': _L0_ffn_in['Ins_tk'], 'L0_ffn_gate_w': _L0_ffn_in['gate_w'], 'L0_ffn_expert_w': _L0_ffn_in['expert_w'], 'L0_ffn_expert_b': _L0_ffn_in['expert_b'], 'L0_ffn_gamma_w': _L0_ffn_in['gamma_w'], 'L0_ffn_beta_w': _L0_ffn_in['beta_w'], 'L0_ffn_rmod_w': _L0_ffn_in['rmod_w'], 'L1_ffn_Wg': _L1_ffn_in['Wg'], 'L1_ffn_W1': _L1_ffn_in['W1'], 'L1_ffn_b1': _L1_ffn_in['b1'], 'L1_ffn_W2': _L1_ffn_in['W2'], 'L1_ffn_b2': _L1_ffn_in['b2']}

def reference(x, L0_tok_g1, L0_tok_b1, L0_tok_Wq, L0_tok_bq, L0_tok_Wk, L0_tok_bk, L0_tok_Wv, L0_tok_bv, L0_tok_Wo, L0_tok_bo, L0_tok_g2, L0_tok_b2, L0_tok_Wf, L0_tok_bf, L0_attn_W, L0_attn_b, L0_ffn_Ins_tk, L0_ffn_gate_w, L0_ffn_expert_w, L0_ffn_expert_b, L0_ffn_gamma_w, L0_ffn_beta_w, L0_ffn_rmod_w, L1_ffn_Wg, L1_ffn_W1, L1_ffn_b1, L1_ffn_W2, L1_ffn_b2):
    import jax
    import jax.numpy as jnp

    def _L0_tok_ref(X, rseq, g1, b1, Wq, bq, Wk, bk, Wv, bv, Wo, bo, g2, b2, Wf, bf):
        import jax, jax.numpy as jnp
        import numpy as np
        D_MODEL = 128
        N_HEADS = 4
        EPS = 1e-05

        def _layernorm(x, g, b):
            m = jnp.mean(x, axis=-1, keepdims=True)
            v = jnp.mean((x - m) ** 2, axis=-1, keepdims=True)
            return (x - m) * jax.lax.rsqrt(v + EPS) * g + b
        d = X.shape[-1]
        X1 = _layernorm(X, g1, b1)
        Xkv = X1[:, :rseq, :]
        Xq = X1[:, rseq:, :]
        Q = jnp.einsum('bqd,hde->bhqe', Xq, Wq) + bq[None, :, None, :]
        K = jnp.einsum('bkd,hde->bhke', Xkv, Wk) + bk[None, :, None, :]
        V = jnp.einsum('bkd,hde->bhke', Xkv, Wv) + bv[None, :, None, :]
        scores = jnp.einsum('bhqe,bhke->bhqk', Q, K) / d ** 0.5
        A = jax.nn.softmax(scores, axis=-1)
        Z = jnp.einsum('bhqk,bhke->bhqe', A, V)
        B, H, Qn, _ = Z.shape
        Z = Z.transpose(0, 2, 1, 3).reshape(B, Qn, H * d)
        Z = Z @ Wo + bo
        Z = Z + Xq
        Z = _layernorm(Z, g2, b2)
        return Z @ Wf + bf

    def _L0_attn_ref(x, W, b):
        import math
        import jax, jax.numpy as jnp
        import numpy as np
        FACTOR = 1
        B, T, D = x.shape
        q = x @ W + b
        qf = q.astype(jnp.float32)
        q_fft = jnp.fft.rfft(qf, axis=1)
        corr_freq = q_fft * jnp.conj(q_fft)
        corr_time = jnp.fft.irfft(corr_freq, n=T, axis=1)
        corr = corr_time.mean(axis=-1)
        topk = min(FACTOR * int(math.log2(T)), T)
        _, delays = jax.lax.top_k(corr, topk)
        idx = (jnp.arange(T)[None, None, :] + delays[:, :, None]) % T
        shifted = jnp.take_along_axis(qf[:, None, :, :], idx[..., None], axis=2)
        context = shifted.mean(axis=1)
        return context + x

    def _L0_ffn_ref(x, Ins_tk, gate_w, expert_w, expert_b, gamma_w, beta_w, rmod_w):
        import jax, jax.numpy as jnp
        import numpy as np
        B, C, IN_LEN, OUT_LEN, E, TOP_K, N_I = (1, 2048, 128, 128, 8, 2, 16)
        Bx, Cx, L = x.shape
        xf = x.reshape(-1, L)
        ins = Ins_tk[0]
        router_gamma = jnp.mean(ins @ rmod_w, axis=0)
        logits = xf @ gate_w + router_gamma
        probs = jax.nn.softmax(logits.astype(jnp.float32), axis=-1)
        rw, sel = jax.lax.top_k(probs, TOP_K)
        combine = jnp.sum(jax.nn.one_hot(sel, E, dtype=rw.dtype) * rw[..., None], axis=1)
        gam = jnp.mean(ins @ gamma_w.T, axis=0)
        bet = jnp.einsum('nh,ehd->ed', ins, beta_w) / N_I
        eo = jnp.einsum('nl,eld->end', xf, expert_w) + expert_b[:, None, :]
        mod = gam[:, None, None] * eo + bet[:, None, :]
        out = jnp.einsum('ne,end->nd', combine, mod)
        return out.reshape(Bx, Cx, OUT_LEN)

    def _L1_attn_ref(x):
        import jax, jax.numpy as jnp
        import numpy as np
        scores = jax.nn.softmax(jnp.einsum('bsd,btd->bst', x, x), axis=-1)
        return jnp.einsum('bst,btd->bsd', scores, x)

    def _L1_ffn_ref(x, Wg, W1, b1, W2, b2):
        import jax, jax.numpy as jnp
        import numpy as np
        B, L, H, E, F, C = (8, 2048, 128, 8, 256, 2)
        b, l, h = x.shape
        e = Wg.shape[1]
        k = min(max(int(l * C / e), 1), l)
        S = jax.nn.softmax(x @ Wg, axis=-1)
        St = jnp.swapaxes(S, 1, 2)
        G, I = jax.lax.top_k(St, k)
        ex = jnp.take_along_axis(x[:, None], I[..., None], axis=2)
        hmid = jax.nn.gelu(jnp.einsum('bekh,ehf->bekf', ex, W1) + b1[None, :, None, :], approximate=False)
        out = jnp.einsum('bekf,efh->bekh', hmid, W2) + b2[None, :, None, :]
        vals = G[..., None] * out
        new_x = jnp.zeros_like(x).at[jnp.arange(b)[:, None, None], I].add(vals)
        return new_x
    h = _L0_tok_ref(x, 128, L0_tok_g1, L0_tok_b1, L0_tok_Wq, L0_tok_bq, L0_tok_Wk, L0_tok_bk, L0_tok_Wv, L0_tok_bv, L0_tok_Wo, L0_tok_bo, L0_tok_g2, L0_tok_b2, L0_tok_Wf, L0_tok_bf)
    h = h + _L0_attn_ref(_layernorm(h, axis=-1), L0_attn_W, L0_attn_b)
    h = h + _L0_ffn_ref(_layernorm(h, axis=-1), L0_ffn_Ins_tk, L0_ffn_gate_w, L0_ffn_expert_w, L0_ffn_expert_b, L0_ffn_gamma_w, L0_ffn_beta_w, L0_ffn_rmod_w)
    h = h + _L1_attn_ref(_layernorm(h, axis=-1))
    h = h + _L1_ffn_ref(_layernorm(h, axis=-1), L1_ffn_Wg, L1_ffn_W1, L1_ffn_b1, L1_ffn_W2, L1_ffn_b2)
    return h

_drawn_inputs = setup_inputs


def setup_inputs(seed=0):
    import zlib

    import numpy as np

    out = dict(_drawn_inputs(seed))
    spreads = {'L0_tok_g1': (1.0, 0.2),
     'L0_tok_b1': (0.0, 0.1),
     'L0_tok_bq': (0.0, 0.1),
     'L0_tok_bk': (0.0, 0.8),
     'L0_tok_bv': (0.0, 0.1),
     'L0_tok_bo': (0.0, 0.1),
     'L0_tok_g2': (1.0, 0.2),
     'L0_tok_b2': (0.0, 0.1),
     'L0_tok_bf': (0.0, 0.1),
     'L0_attn_b': (0.0, 0.1),
     'L0_ffn_expert_b': (0.0, 0.8),
     'L1_ffn_b1': (0.0, 0.8),
     'L1_ffn_b2': (0.0, 0.549)}
    factors = {'L0_ffn_Ins_tk': 7.308,
     'L0_ffn_gate_w': 8.0,
     'L0_ffn_expert_w': 8.0,
     'L0_ffn_gamma_w': 8.0,
     'L0_ffn_beta_w': 7.581,
     'L0_ffn_rmod_w': 8.0}
    for name, (base, spread) in spreads.items():
        noise = np.random.default_rng([zlib.crc32(name.encode()), seed]).standard_normal(out[name].shape)
        drawn = base * np.exp(spread * noise) if base else spread * noise
        out[name] = jnp.asarray(drawn.astype(out[name].dtype))
    for name, factor in factors.items():
        out[name] = (out[name] * factor).astype(out[name].dtype)
    return out
```

```python
from contextlib import ExitStack

import concourse.bass as bass
from concourse import mybir

F32 = mybir.dt.float32
ALU = mybir.AluOpType
ACT = mybir.ActivationFunctionType
AX = mybir.AxisListType

EPS = 1e-5
LOWEST = -3e38
TAKEN = 3e38
CHOSEN = -2e38
SHIFT = 64.0


def is_live(b, n):
    return not isinstance(b, int) or 0 <= b < n


def wait(eng, sem, value):
    if not isinstance(value, int) or value > 0:
        eng.wait_ge(sem, value)


def wait_apart(eng, sem, value, met):
    if isinstance(value, int):
        eng.wait_ge(sem, value)
    else:
        register = eng.to_reg(value)
        eng.wait_ge(met, 1)
        eng.wait_ge(sem, register)


def dma_count(b, slot, slots, per):
    if isinstance(b, int):
        return (b // slots + 1) * per
    return (b - slot) * (per // slots) + per


def walk(eng, n, lead, unroll, tail, step):
    assert lead % unroll == 0 and (n - lead) % unroll == 0 and n > lead
    for t in range(lead):
        step(t, t % unroll)
    with eng.Fori(lead, n - unroll + 1, unroll) as t:
        for r in range(unroll):
            step(t + r, r)
    for t in range(n, n + tail):
        step(t, t % unroll)


def audio_tower(nc, x, tab_fwd_cos, tab_fwd_sin, tab_inv_cos, tab_inv_sin,
                g1, b1, Wq, bq, Wk, bk, Wv, bv, Wo, bo, g2, b2, Wf, bf,
                Wa, ba, ins, gate_w, expert_w, expert_b, gamma_w, beta_w, rmod_w,
                Wg, W1, eb1, W2, eb2, out):
    N, S, D = x.shape
    H = Wq.shape[0]
    T = out.shape[1]
    KV = S - T
    C = 2
    P = (T + C - 1) // C
    TP = C * P
    LAST = T - P
    NI = ins.shape[1]
    E = gate_w.shape[1]
    F = W1.shape[2]
    FC = F // D
    K = min(max(T * 2 // E, 1), T)
    DELAYS = 1
    while 2 ** (DELAYS + 1) <= T:
        DELAYS += 1
    NF = T // 2 + 1
    PAIRS = (DELAYS - 1) // 2
    assert D == 128 and KV == 128 and T % 2 == 1 and DELAYS % 2 == 1 and NF == P and N <= 128
    assert E == 8 and N % 16 == 0 or N == 24
    SCALE = float(D) ** -0.5
    EK = E * K
    NB = 4
    KB = EK // NB
    Q4 = 4
    U, LEAD, TAIL = 4, 8, 6
    UE, LEADE, TAILE = 8, 16, 9

    with ExitStack() as ctx:
        def sb(name, shape, dt=F32):
            return ctx.enter_context(nc.sbuf_tensor(name, shape, dt))

        def sem(name):
            return ctx.enter_context(nc.semaphore(name))

        bank = [ctx.enter_context(nc.psum_tensor(f"bank{i}", [128, 512], F32)) for i in range(8)]

        h = sb("h", [P, N, C, D])
        wide = sb("wide", [128, 64 * 256])
        narrow = sb("narrow", [128, 5600])
        ident = sb("ident", [128, 128])
        fwd = sb("fwd", [P, 2, C, NF])
        inv = sb("inv", [NF, 2, TP])
        wq = sb("wq", [D, H, D])
        wk = sb("wk", [D, H, D])
        wvo = sb("wvo", [D, H, D])
        wf = sb("wf", [D, D])
        wa = sb("wa", [D, D])
        wx = sb("wx", [D, E, D])
        gatew = sb("gatew", [D, E])
        wg = sb("wg", [D, E])
        w1 = sb("w1", [D, E, F])
        w2 = sb("w2", [D, E, FC, D])
        cols = sb("cols", [D, 4 + 2 * H])
        b1col = sb("b1col", [D, E, FC])
        b2col = sb("b2col", [D, E])
        g1row = sb("g1row", [P, D])
        bfrow = sb("bfrow", [P, D])
        barow = sb("barow", [P, D])
        crow = sb("crow", [P, D])
        rgrow = sb("rgrow", [P, E])
        bmod = sb("bmod", [C * E, C, D])
        slotno = sb("slotno", [P, K])
        mhalf = sb("mhalf", [128, 4])
        epsilon = sb("epsilon", [128, 4])
        mshift = sb("mshift", [128, 1])
        power = sb("power", [NF, N])
        wfreq = sb("wfreq", [NF, N])
        gates = sb("gates", [P, C, N * E])
        slots = sb("slots", [P, C, N * E])

        taken = {}

        def carve(tensor, start=0):
            taken[0] = start

            def piece(parts, *shape):
                size = 1
                for s in shape:
                    size *= s
                at = taken[0]
                taken[0] = at + size
                assert at + size <= tensor.shape[1], (at + size, tensor.shape)
                ap = tensor[0:parts, at:at + size]
                names = "abcd"[:len(shape)]
                if len(shape) == 1:
                    return ap
                return ap.rearrange(f"p ({' '.join(names)}) -> p {' '.join(names)}",
                                    **{k: s for k, s in zip(names[1:], shape[1:])})
            return piece

        block = ctx.enter_context(nc.Block())

        w_prep = sem("w_prep")
        w_main = sem("w_main")
        w_zero = sem("w_zero")
        w_eb = sem("w_eb")
        c_set = sem("c_set")
        c_set2 = sem("c_set2")
        p_mm = sem("p_mm")
        p_cp = sem("p_cp")

        a_in = [sem(f"a_in{i}") for i in range(2)]
        (a_bn, a_mv, a_ve, a_rstd, a_xn, a_res0, a_res, a_T, a_xT, a_Q, a_Qe, a_K, a_Ke, a_V, a_Ve,
         a_S, a_mx, a_sub, a_exp, a_sum, a_rcp, a_An, a_AT, a_ATe, a_AV, a_y) = [
            sem(s) for s in ("a_bn a_mv a_ve a_rstd a_xn a_res0 a_res a_T a_xT a_Q a_Qe a_K a_Ke a_V a_Ve "
                             "a_S a_mx a_sub a_exp a_sum a_rcp a_An a_AT a_ATe a_AV a_y").split()]
        (b_bn, b_mv, b_ve, b_rstd, b_yn, b_T, b_ynT, b_H, b_h, b_bn2, b_mv2, b_ve2, b_rstd2, b_x, b_res,
         b_T2, b_xT, b_Q, b_q, b_F, b_pw, b_P) = [
            sem(s) for s in ("b_bn b_mv b_ve b_rstd b_yn b_T b_ynT b_H b_h b_bn2 b_mv2 b_ve2 b_rstd2 b_x b_res "
                             "b_T2 b_xT b_Q b_q b_F b_pw b_P").split()]
        k_mm, k_cp, k_own = sem("k_mm"), sem("k_cp"), sem("k_own")
        (c_G, c_I, c_h, c_bn, c_mv, c_ve, c_rstd, c_x, c_T, c_xT, c_L, c_lg, c_m8, c_sel, c_mr, c_sub, c_exp,
         c_sum, c_rcp, c_cu, c_c, c_CT, c_cT, c_B, c_hb, c_E, c_stt, c_act, c_add1, c_add2, c_out) = [
            sem(s) for s in ("c_G c_I c_h c_bn c_mv c_ve c_rstd c_x c_T c_xT c_L c_lg c_m8 c_sel c_mr c_sub "
                             "c_exp c_sum c_rcp c_cu c_c c_CT c_cT c_B c_hb c_E c_stt c_act c_add1 c_add2 "
                             "c_out").split()]
        (d_bn, d_mv, d_ve, d_rstd, d_x, d_T, d_xT, d_G, d_E, d_O, d_rcp, d_h, d_bn2, d_mv2, d_ve2, d_rstd2,
         d_x2, d_T2, d_xT2, d_L, d_mx, d_sub, d_exp, d_sum, d_rcp2, d_S) = [
            sem(s) for s in ("d_bn d_mv d_ve d_rstd d_x d_T d_xT d_G d_E d_O d_rcp d_h d_bn2 d_mv2 d_ve2 "
                             "d_rstd2 d_x2 d_T2 d_xT2 d_L d_mx d_sub d_exp d_sum d_rcp2 d_S").split()]
        (t_mm, t_cp, t_top, t_mr, t_mask, t_scan, t_id0, t_id, t_mm2, t_slot, t_set) = [
            sem(s) for s in "t_mm t_cp t_top t_mr t_mask t_scan t_id0 t_id t_mm2 t_slot t_set".split()]
        (e_bn, e_mv, e_ve, e_rstd, e_x, e_P, e_PG, e_X, e_xe, e_PT, e_PTe, e_H, e_hm, e_V, e_v, e_VT, e_vt,
         e_O, e_o) = [
            sem(s) for s in ("e_bn e_mv e_ve e_rstd e_x e_P e_PG e_X e_xe e_PT e_PTe e_H e_hm e_V e_v e_VT "
                             "e_vt e_O e_o").split()]
        e_out = [sem(f"e_out{i}") for i in range(2)]

        piece = carve(wide, 11376)
        wv = piece(D, H, D)
        wo = piece(D, H, D)
        wvT = piece(D, H, D)
        bvcol = piece(D, H)
        bvwide = piece(D, H, P)
        insT = piece(NI, D)
        ninv = piece(NI, 1)
        insmean = piece(D, 1)
        inswide = piece(D, D)
        inssel = piece(D, C * E * C * E)
        rmod = piece(D, E)
        gam_w = piece(E, D)
        gamT = piece(D, C, E)
        gamrow = piece(D, E)
        gamcol = piece(C * E, 1)
        beta = piece(D, E, D)
        ebz = piece(C * E, C, D)
        borow = piece(P, D)
        b1row = piece(P, D)

        piece = carve(wide)
        A_xn = [piece(128, 3, D) for _ in range(2)]
        A_xT = [piece(D, KV + TP) for _ in range(2)]
        A_QT = [piece(D, H, TP) for _ in range(2)]
        A_KT = [piece(D, H, KV) for _ in range(2)]
        A_xk = [piece(KV, D) for _ in range(2)]
        A_xq = [piece(P, C, D) for _ in range(2)]
        A_V = [piece(KV, H, D) for _ in range(4)]
        A_A = [[piece(P, H, KV) for _ in range(C)] for _ in range(2)]
        A_AT = [piece(KV, C, H, P) for _ in range(2)]
        assert taken[0] <= 11376
        piece = carve(narrow)
        A_st = [piece(128, 3, 6) for _ in range(2)]
        A_mv = [piece(128, 3, 2) for _ in range(2)]
        A_ve = [piece(128, 3) for _ in range(2)]
        A_rstd = [piece(128, 3) for _ in range(2)]
        A_mx = [piece(P, C, H) for _ in range(2)]
        A_sm = [piece(P, C, H) for _ in range(2)]
        A_rc = [piece(P, C, H) for _ in range(2)]

        B_st = [piece(P, C, 6) for _ in range(2)]
        B_mv = [piece(P, C, 2) for _ in range(2)]
        B_ve = [piece(P, C) for _ in range(2)]
        B_rstd = [piece(P, C) for _ in range(2)]
        B_st2 = [piece(P, C, 6) for _ in range(2)]
        B_mv2 = [piece(P, C, 2) for _ in range(2)]
        B_ve2 = [piece(P, C) for _ in range(2)]
        B_rstd2 = [piece(P, C) for _ in range(2)]
        B_pw = [piece(NF, 1) for _ in range(2)]
        B_yn = [piece(P, C, D) for _ in range(2)]
        B_ynT = [piece(D, TP) for _ in range(2)]
        B_h = [piece(P, C, D) for _ in range(2)]
        B_x = [piece(P, C, D) for _ in range(2)]
        B_xT = [piece(D, TP) for _ in range(2)]
        B_q = [piece(P, C, D) for _ in range(2)]
        B_junk = piece(NF, 2 * D)
        spectra = wide[0:NF, 0:N * 2 * D].rearrange("p (n r d) -> p n r d", n=N, r=2)

        piece = carve(narrow)
        K_cr = piece(N, NF - 1 + 8 - PAIRS)
        K_m8 = piece(N, 8)
        K_sel = piece(N, 8)
        K_mr = piece(N, NF - 1 + 8 - PAIRS)
        K_w = piece(N, NF)
        K_wT = piece(NF, N)

        piece = carve(narrow)
        C_st = [piece(P, C, 6) for _ in range(2)]
        C_mv = [piece(P, C, 2) for _ in range(2)]
        C_ve = [piece(P, C) for _ in range(2)]
        C_rstd = [piece(P, C) for _ in range(2)]
        C_lg = [piece(P, C, E + 6) for _ in range(2)]
        C_m8 = [piece(P, C, 8) for _ in range(2)]
        C_sel = [piece(P, C, 8) for _ in range(2)]
        C_mr = [piece(P, C, E + 6) for _ in range(2)]
        C_ex = [piece(P, C, E) for _ in range(2)]
        C_sm = [piece(P, C) for _ in range(2)]
        C_rc = [piece(P, C) for _ in range(2)]
        C_c = [piece(P, C, E) for _ in range(2)]
        C_cT = [piece(C * E, P) for _ in range(2)]
        C_G = [piece(NF, 2, D) for _ in range(2)]
        C_h = [piece(P, C, D) for _ in range(4)]
        C_x = [piece(P, C, D) for _ in range(2)]
        C_xT = [piece(D, TP) for _ in range(4)]
        C_t = piece(P, C, E // 2, D)
        C_u = piece(P, C, 2, D)

        piece = carve(narrow)
        D_st = [piece(P, C, 6) for _ in range(2)]
        D_mv = [piece(P, C, 2) for _ in range(2)]
        D_ve = [piece(P, C) for _ in range(2)]
        D_rstd = [piece(P, C) for _ in range(2)]
        D_st2 = [piece(P, C, 6) for _ in range(2)]
        D_mv2 = [piece(P, C, 2) for _ in range(2)]
        D_ve2 = [piece(P, C) for _ in range(2)]
        D_rstd2 = [piece(P, C) for _ in range(2)]
        D_rc = [piece(P, C) for _ in range(2)]
        D_mx = [piece(P, C) for _ in range(2)]
        D_sm = [piece(P, C) for _ in range(2)]
        D_rc2 = [piece(P, C) for _ in range(2)]
        D_lg = [piece(P, C, E) for _ in range(2)]
        D_x = [piece(P, C, D + 1) for _ in range(4)]
        D_xT = [piece(D, TP) for _ in range(2)]
        D_E = [piece(P, C, TP) for _ in range(2)]
        D_x2 = [piece(P, C, D) for _ in range(2)]
        D_xT2 = [piece(D, TP) for _ in range(2)]

        GB = 128 // E
        NG = (N + GB - 1) // GB
        piece = carve(narrow)
        T_s = [piece(128, T + 3) for _ in range(2)]
        T_w = [piece(128, T + 3) for _ in range(2)]
        T_m8 = [piece(128, 8) for _ in range(2)]
        T_pos = [piece(128, T) for _ in range(2)]
        T_id = [piece(128, TP) for _ in range(2)]
        T_one = piece(128, T)

        piece = carve(wide)
        E_PT = [piece(KB, C, NB, P) for _ in range(8)]
        E_xe = [piece(D, E, Q4, K) for _ in range(2)]
        E_vt = [piece(D, Q4, E, K) for _ in range(2)]
        piece = carve(narrow)
        E_st = [piece(P, C, 6) for _ in range(2)]
        E_mv = [piece(P, C, 2) for _ in range(2)]
        E_ve = [piece(P, C) for _ in range(2)]
        E_rstd = [piece(P, C) for _ in range(2)]
        E_x = [piece(P, C, D) for _ in range(2)]
        E_P = [piece(P, C, E, K) for _ in range(2)]
        E_PG = [piece(P, C, E, K) for _ in range(1)]
        E_hm = [piece(D, FC, Q4 * K) for _ in range(2)]
        E_v = piece(KB, NB, D)
        def rows(ap, parts):
            return ap.partition_broadcast(parts)

        @block.sync
        def _(sp):
            prep = [(wv, Wv.rearrange("h d e -> d h e")), (wo, Wo.rearrange("(h e) d -> e h d", h=H)),
                    (bvcol, bv.rearrange("h e -> e h")), (insT, ins[0]),
                    (rmod, rmod_w), (gam_w, gamma_w), (beta, beta_w.rearrange("e h d -> h e d")),
                    (borow, rows(bo, P)), (b1row, rows(b1, P)),
                    (wx[:, :, :], expert_w.rearrange("e l d -> l e d"))]
            for dst, src in prep:
                sp.dma_start(dst, src, allow_slow_non_contiguous=True).then_inc(w_prep, 16)
            main = [(wq[:, :, :], Wq.rearrange("h d e -> d h e")), (wk[:, :, :], Wk.rearrange("h d e -> d h e")),
                    (cols[:, 0:1], g1.unsqueeze(1)), (cols[:, 1:2], b1.unsqueeze(1)),
                    (cols[:, 2:3], g2.unsqueeze(1)), (cols[:, 3:4], b2.unsqueeze(1)),
                    (cols[:, 4:4 + H], bq.rearrange("h e -> e h")), (cols[:, 4 + H:4 + 2 * H], bk.rearrange("h e -> e h")),
                    (g1row[:, :], rows(g1, P)), (bfrow[:, :], rows(bf, P)), (barow[:, :], rows(ba, P)),
                    (wf[:, :], Wf), (wa[:, :], Wa), (gatew[:, :], gate_w), (wg[:, :], Wg),
                    (fwd[:, 0, :, :], tab_fwd_cos.rearrange("(c p) f -> p c f", c=C)),
                    (fwd[:, 1, :, :], tab_fwd_sin.rearrange("(c p) f -> p c f", c=C)),
                    (inv[:, 0, :], tab_inv_cos), (inv[:, 1, :], tab_inv_sin),
                    (w1[:, :, :], W1.rearrange("e d f -> d e f")),
                    (w2[:, :, :, :], W2.rearrange("e (c f) d -> f e c d", c=FC)),
                    (b1col[:, :, :], eb1.rearrange("e (c f) -> f e c", c=FC)),
                    (b2col[:, :], eb2.rearrange("e d -> d e"))]
            for dst, src in main:
                sp.dma_start(dst, src, allow_slow_non_contiguous=True).then_inc(w_main, 16)
            sp.wait_ge(w_zero, 1)
            for c in range(C):
                sp.dma_start(ebz[c * E:(c + 1) * E, c, :], expert_b).then_inc(w_eb, 16)

            def load(t, r):
                if not is_live(t, N):
                    return
                s = r % 2
                wait(sp, a_xn, t - 1)
                if isinstance(t, int) and t < 2:
                    sp.wait_ge(c_set, 1)
                sp.dma_start(A_xk[s], x[t, 0:KV, :]).then_inc(a_in[s], 16)
                for c in range(C):
                    m = P if c < C - 1 else LAST
                    sp.dma_start(A_xq[s][0:m, c, :], x[t, KV + c * P:KV + c * P + m, :]).then_inc(a_in[s], 16)
            walk(sp, N, LEAD, U, 0, load)

            def store(t, r):
                b = t - 9
                if not is_live(b, N):
                    return
                s = (r - 9) % 2
                wait(sp, e_o, b + 1)
                for c in range(C):
                    m = P if c < C - 1 else LAST
                    sp.dma_start(out[b, c * P:c * P + m, :], h[0:m, b, c, :]).then_inc(e_out[s], 16)
            walk(sp, N, LEADE, UE, TAILE, store)
            for s in range(2):
                sp.wait_ge(e_out[s], 16 * C * (N // 2))

        @block.gpsimd
        def _(pool):
            for s in range(2):
                nc.gpsimd.memset(A_xq[s], 0.0)
            nc.gpsimd.memset(epsilon[:, :], EPS)
            nc.gpsimd.memset(mhalf[:, :], -0.5).then_inc(c_set, 1)
            nc.gpsimd.memset(ebz, 0.0).then_inc(w_zero, 1)
            nc.gpsimd.memset(mshift[:, :], -SHIFT)
            nc.gpsimd.memset(inssel, 0.0)
            nc.gpsimd.memset(ninv, 1.0 / NI)
            for s in range(2):
                nc.gpsimd.memset(A_mv[s], 1.0)
            nc.gpsimd.iota(slotno[:, :], [[1, K]], base=0, channel_multiplier=0,
                           allow_small_or_imprecise_dtypes=True)
            nc.gpsimd.memset(ident[:, :], 0.0).then_inc(c_set, 1)
            pool.wait_ge(c_set, 2)
            nc.gpsimd.affine_select(out=ident[:, :], in_=ident[:, :], compare_op=ALU.not_equal, fill=1.0, base=0,
                                    pattern=[[-1, 128]], channel_multiplier=1).then_inc(c_set, 1)
            pool.wait_ge(w_prep, 16 * 10)
            nc.gpsimd.tensor_tensor(b1row, b1row, borow, ALU.add).then_inc(c_set, 1)

            def root(b, r, var, ve, rstd, e_sem, r_sem, n_mv, freed):
                pool.wait_ge(n_mv, b + 1)
                wait(pool, freed, b - 1)
                nc.gpsimd.tensor_tensor(ve, var, epsilon[0:ve.shape[0], 0:ve.shape[1]], ALU.add).then_inc(e_sem, 1)
                pool.wait_ge(e_sem, b + 1)
                nc.gpsimd.tensor_tensor(rstd, ve, mhalf[0:ve.shape[0], 0:ve.shape[1]], ALU.pow).then_inc(r_sem, 1)

            def phase_a(t, r):
                if is_live(t, N):
                    s = r % 2
                    root(t, r, A_mv[s][:, :, 1], A_ve[s], A_rstd[s], a_ve, a_rstd, a_mv, a_xn)
                    wait_apart(pool, a_xn, t + 1, c_set)
                    if isinstance(t, int) and t == 0:
                        pool.wait_ge(w_main, 16 * 23)
                        pool.wait_ge(p_cp, 5)
                    nc.gpsimd.tensor_tensor(h[:, t], A_xn[s][0:P, 1:3, :],
                                            g1row[:, :].unsqueeze(1).broadcast_to([P, C, D]),
                                            ALU.mult).then_inc(a_res0, 1)
                    wait_apart(pool, a_res0, t + 1, c_set)
                    nc.gpsimd.tensor_tensor(h[:, t], h[:, t], crow[:, :].unsqueeze(1).broadcast_to([P, C, D]),
                                            ALU.add).then_inc(a_res, 1)
                b = t - 3
                if is_live(b, N):
                    s = (r - 3) % 2
                    pool.wait_ge(a_rcp, b + 1)
                    for c in range(C):
                        nc.gpsimd.tensor_tensor(A_A[s][c], A_A[s][c],
                                                A_rc[s][:, c, :].unsqueeze(2).broadcast_to([P, H, KV]),
                                                ALU.mult).then_inc(a_An, 1)
            walk(pool, N, LEAD, U, TAIL, phase_a)

            def phase_b(t, r):
                if is_live(t, N):
                    s = r % 2
                    root(t, r, B_mv[s][:, :, 1], B_ve[s], B_rstd[s], b_ve, b_rstd, b_mv, b_yn)
                b = t - 2
                if is_live(b, N):
                    s = (r - 2) % 2
                    root(b, r, B_mv2[s][:, :, 1], B_ve2[s], B_rstd2[s], b_ve2, b_rstd2, b_mv2, b_x)
                b = t - 3
                if is_live(b, N):
                    s = (r - 3) % 2
                    wait_apart(pool, b_x, b + 1, c_set)
                    nc.gpsimd.tensor_tensor(h[:, b], B_h[s], B_x[s], ALU.add).then_inc(b_res, 1)
                b = t - 5
                if is_live(b, N):
                    s = (r - 5) % 2
                    wait_apart(pool, b_pw, b + 1, c_set)
                    nc.gpsimd.tensor_copy(power[:, b:b + 1] if isinstance(b, int) else power[:, bass.ds(b, 1)],
                                          B_pw[s]).then_inc(b_P, 1)
            walk(pool, N, LEAD, U, TAIL, phase_b)

            def phase_c(t, r):
                b = t - 1
                if is_live(b, N):
                    s = (r - 1) % 2
                    root(b, r, C_mv[s][:, :, 1], C_ve[s], C_rstd[s], c_ve, c_rstd, c_mv, c_x)
                b = t - 4
                if is_live(b, N):
                    pool.wait_ge(c_act, C * (b + 1))
                    wait(pool, c_out, b)
                    half = E // 4
                    nc.gpsimd.tensor_tensor(C_u, C_t[:, :, 0:half, :], C_t[:, :, half:, :], ALU.add)\
                        .then_inc(c_add1, 1)
                    pool.wait_ge(c_add1, b + 1)
                    nc.gpsimd.tensor_tensor(C_u[:, :, 0, :], C_u[:, :, 0, :], C_u[:, :, 1, :], ALU.add)\
                        .then_inc(c_add2, 1)
            walk(pool, N, LEAD, U, TAIL, phase_c)

            def phase_d(t, r):
                if is_live(t, N):
                    s = r % 2
                    root(t, r, D_mv[s][:, :, 1], D_ve[s], D_rstd[s], d_ve, d_rstd, d_mv, d_x)
                b = t - 3
                if is_live(b, N):
                    s = (r - 3) % 2
                    root(b, r, D_mv2[s][:, :, 1], D_ve2[s], D_rstd2[s], d_ve2, d_rstd2, d_mv2, d_x2)
            walk(pool, N, LEAD, U, TAIL, phase_d)

            def phase_e(t, r):
                if is_live(t, N):
                    s = r % 2
                    root(t, r, E_mv[s][:, :, 1], E_ve[s], E_rstd[s], e_ve, e_rstd, e_mv, e_x)
                    wait_apart(pool, e_P, C * (t + 1), c_set)
                    wait(pool, e_PT, C * t)
                    for c in range(C):
                        gate = gates[:, c, E * t:E * t + E] if isinstance(t, int) else gates[:, c, bass.ds(t * E, E)]
                        nc.gpsimd.tensor_tensor(E_PG[0][:, c], E_P[s][:, c],
                                                gate.unsqueeze(2).broadcast_to([P, E, K]),
                                                ALU.mult).then_inc(e_PG, 1)
            walk(pool, N, LEADE, UE, 0, phase_e)

        @block.tensor
        def _(pe):
            mm, tr = nc.tensor.matmul, nc.tensor.transpose

            pe.wait_ge(c_set, 4)
            pe.wait_ge(w_prep, 16 * 10)
            for i in range(H):
                last = tr(bank[0][:, i * D:(i + 1) * D], wv[:, i, :], ident[:, :])
            last.then_inc(p_mm, 1)
            mm(bank[1][:, 0:1], insT, ninv, start=True, stop=True)
            tr(bank[2][:, 0:E], gam_w, ident[0:E, 0:E]).then_inc(p_mm, 1)
            pe.wait_ge(p_cp, 4)
            for i in range(H):
                mm(bank[3][0:P, 0:D], bvwide[:, i, :], wo[:, i, :], start=(i == 0), stop=(i == H - 1))
            for i in range(H):
                last = mm(bank[4][:, i * D:(i + 1) * D], wvT[:, i, :], wo[:, i, :], start=True, stop=True)
            last.then_inc(p_mm, 1)
            mm(bank[5][0:P, 0:E], inswide[:, 0:P], rmod, start=True, stop=True)
            mm(bank[5][0:C * E, 16:17], gamT.rearrange("p c e -> p (c e)"), insmean, start=True, stop=True)
            mm(bank[6][:, 0:E], inswide, gamT[:, 0, :], start=True, stop=True)
            for c in range(C):
                for e in range(E):
                    at = (c * E + e) * C * E
                    last = mm(bank[7][0:C * E, c * D:(c + 1) * D], inssel[:, at:at + C * E], beta[:, e, :],
                              start=(e == 0), stop=(e == E - 1))
            last.then_inc(p_mm, 1)

            def phase_a(t, r):
                if isinstance(t, int) and t == 0:
                    pe.wait_ge(w_main, 16 * 23)
                    pe.wait_ge(p_cp, 10)
                b = t - 2
                if is_live(b, N):
                    s = (r - 2) % 2
                    pe.wait_ge(a_xT, b + 1)
                    for i in range(H):
                        if i == 0:
                            wait(pe, a_Qe, 2 * b - 1)
                            wait(pe, a_ATe, 2 * (b - 2))
                        if i == H // 2:
                            wait(pe, a_Qe, 2 * b)
                            wait(pe, a_y, b - 3)
                        last = mm(bank[1 + i // 2][:, (i % 2) * TP:(i % 2 + 1) * TP], wq[:, i, :],
                                  A_xT[s][:, KV:], start=True, stop=True)
                        if i % 2 == 1:
                            last.then_inc(a_Q, 1)
                b = t - 3
                if is_live(b, N):
                    s = (r - 3) % 2
                    pe.wait_ge(a_Qe, 2 * b + 2)
                    pe.wait_ge(a_Ke, b + 1)
                    for c in range(C):
                        wait(pe, a_sub, 2 * b + c - 1)
                        for i in range(H):
                            last = mm(bank[5 + c][0:P, i * KV:(i + 1) * KV], A_QT[s][:, i, c * P:(c + 1) * P],
                                      A_KT[s][:, i, :], start=True, stop=True)
                        last.then_inc(a_S, 1)
                b = t - 1
                if is_live(b, N):
                    s = (r - 1) % 2
                    pe.wait_ge(a_xn, b + 1)
                    wait(pe, a_xT, b)
                    tr(bank[0][:, 0:KV], A_xn[s][:, 0, :], ident[:, :])
                    for c in range(C):
                        last = tr(bank[0][:, KV + c * P:KV + (c + 1) * P], A_xn[s][0:P, 1 + c, :], ident[0:P, 0:P])
                    last.then_inc(a_T, 1)
                b = t - 4
                if is_live(b, N):
                    s = (r - 4) % 2
                    for c in range(C):
                        pe.wait_ge(a_An, 2 * b + c + 1)
                        wait(pe, a_ATe, 2 * b - 1 + c)
                        if c == 1:
                            pe.wait_ge(a_Qe, min(2 * b + 5, 2 * N) if isinstance(b, int) else 2 * b + 5)
                        for i in range(H):
                            last = tr(bank[7 if c == 0 else 1][:, i * P:(i + 1) * P], A_A[s][c][:, i, :],
                                      ident[0:P, 0:P])
                        last.then_inc(a_AT, 1)
                b = t - 5
                if is_live(b, N):
                    s = (r - 5) % 2
                    pe.wait_ge(a_ATe, 2 * b + 2)
                    pe.wait_ge(a_Ve, b + 1)
                    pe.wait_ge(a_Qe, min(2 * b + 8, 2 * N) if isinstance(b, int) else 2 * b + 8)
                    wait(pe, a_y, b)
                    for c in range(C):
                        for i in range(H):
                            last = mm(bank[2][0:P, c * D:(c + 1) * D], A_AT[s][:, c, i, :],
                                      A_V[(r - 5) % 4][:, i, :], start=(i == 0), stop=(i == H - 1))
                    last.then_inc(a_AV, 1)
                b = t - 2
                if is_live(b, N):
                    s = (r - 2) % 2
                    wait(pe, a_Ke, b)
                    for i in range(H):
                        last = mm(bank[3][:, i * KV:(i + 1) * KV], wk[:, i, :], A_xT[s][:, 0:KV],
                                  start=True, stop=True)
                    last.then_inc(a_K, 1)
                    wait(pe, a_Ve, b)
                    mm(bank[4][:, :], A_xT[s][:, 0:KV], wvo[:, :, :].rearrange("p h d -> p (h d)"),
                       start=True, stop=True).then_inc(a_V, 1)
            walk(pe, N, LEAD, U, TAIL, phase_a)

            def phase_b(t, r):
                if isinstance(t, int) and t == 0:
                    pe.wait_ge(a_y, N)
                b = t - 2
                if is_live(b, N):
                    s = (r - 2) % 2
                    pe.wait_ge(b_ynT, b + 1)
                    wait(pe, b_h, b)
                    for c in range(C):
                        last = mm(bank[1][0:P, c * D:(c + 1) * D], B_ynT[s][:, c * P:(c + 1) * P], wf[:, :],
                                  start=True, stop=True)
                    last.then_inc(b_H, 1)
                b = t - 4
                if is_live(b, N):
                    s = (r - 4) % 2
                    pe.wait_ge(b_xT, b + 1)
                    wait(pe, b_q, b)
                    for c in range(C):
                        last = mm(bank[3][0:P, c * D:(c + 1) * D], B_xT[s][:, c * P:(c + 1) * P], wa[:, :],
                                  start=True, stop=True)
                    last.then_inc(b_Q, 1)
                b = t - 5
                if is_live(b, N):
                    s = (r - 5) % 2
                    pe.wait_ge(b_q, b + 1)
                    wait(pe, b_pw, b)
                    for k in range(2):
                        for c in range(C):
                            last = mm(bank[4][0:NF, k * D:(k + 1) * D], fwd[:, k, c, :], B_q[s][:, c, :],
                                      start=(c == 0), stop=(c == C - 1))
                    last.then_inc(b_F, 1)
                b = t - 1
                if is_live(b, N):
                    s = (r - 1) % 2
                    pe.wait_ge(b_yn, b + 1)
                    wait(pe, b_ynT, b)
                    for c in range(C):
                        last = tr(bank[0][:, c * P:(c + 1) * P], B_yn[s][:, c, :], ident[0:P, 0:P])
                    last.then_inc(b_T, 1)
                b = t - 3
                if is_live(b, N):
                    s = (r - 3) % 2
                    pe.wait_ge(b_x, b + 1)
                    wait(pe, b_xT, b)
                    for c in range(C):
                        last = tr(bank[2][:, c * P:(c + 1) * P], B_x[s][:, c, :], ident[0:P, 0:P])
                    last.then_inc(b_T2, 1)
            walk(pe, N, LEAD, U, TAIL, phase_b)

            pe.wait_ge(b_P, N)
            mm(bank[5][0:N, 0:NF], power[:, :], inv[:, 0, 0:NF], start=True, stop=True).then_inc(k_mm, 1)
            pe.wait_ge(k_cp, 5)
            tr(bank[6][0:NF, 0:N], K_w, ident[0:N, 0:N]).then_inc(k_mm, 1)
            pe.wait_ge(k_cp, 6)
            mm(bank[7][0:NF, 0:N], fwd[:, 0, 0, :], K_wT, start=True, stop=True).then_inc(k_mm, 1)

            def phase_c(t, r):
                if isinstance(t, int) and t == 0:
                    pe.wait_ge(k_cp, 7)
                b = t - 1
                if is_live(b, N):
                    s = (r - 1) % 2
                    pe.wait_ge(c_G, b + 1)
                    wait(pe, c_h, b)
                    for c in range(C):
                        for k in range(2):
                            last = mm(bank[0][0:P, c * D:(c + 1) * D], inv[:, k, c * P:(c + 1) * P],
                                      C_G[s][:, k, :], start=(k == 0), stop=(k == 1))
                    last.then_inc(c_I, 1)
                b = t - 3
                if is_live(b, N):
                    s = (r - 3) % 4
                    pe.wait_ge(c_xT, b + 1)
                    wait(pe, c_lg, b)
                    for c in range(C):
                        last = mm(bank[2][0:P, c * E:(c + 1) * E], C_xT[s][:, c * P:(c + 1) * P], gatew[:, :],
                                  start=True, stop=True)
                    last.then_inc(c_L, 1)
                b = t - 4
                if is_live(b, N):
                    s = (r - 4) % 2
                    for c in range(C):
                        for k in range(2):
                            if k == 0:
                                wait(pe, c_stt, E * b - 1 + c)
                            else:
                                wait(pe, c_act, C * (b - 1) + c + 1)
                            mm(bank[3 + 2 * c + k][0:P, :], C_xT[(r - 4) % 4][:, c * P:(c + 1) * P],
                               wx[:, k * E // 2:(k + 1) * E // 2, :].rearrange("p e d -> p (e d)"),
                               start=True, stop=True).then_inc(c_E, 1)
                        if c == 0:
                            pe.wait_ge(c_c, b + 1)
                            wait(pe, c_hb, b)
                            tr(bank[7][0:C * E, 0:P], C_c[s].rearrange("p c e -> p (c e)"), ident[0:P, 0:P])\
                                .then_inc(c_CT, 1)
                    pe.wait_ge(c_cT, b + 1)
                    for c in range(C):
                        last = mm(bank[7][0:P, 128 + c * D:128 + (c + 1) * D], C_cT[s], bmod[:, c, :],
                                  start=True, stop=True)
                    last.then_inc(c_B, 1)
                b = t - 2
                if is_live(b, N):
                    s = (r - 2) % 2
                    pe.wait_ge(c_x, b + 1)
                    wait(pe, c_xT, b)
                    for c in range(C):
                        last = tr(bank[1][:, c * P:(c + 1) * P], C_x[s][:, c, :], ident[0:P, 0:P])
                    last.then_inc(c_T, 1)
            walk(pe, N, LEAD, U, TAIL, phase_c)

            def phase_d(t, r):
                if isinstance(t, int) and t == 0:
                    pe.wait_ge(c_out, N)
                b = t - 2
                if is_live(b, N):
                    s = (r - 2) % 2
                    pe.wait_ge(d_xT, b + 1)
                    wait(pe, d_E, b)
                    for c in range(C):
                        last = mm(bank[1][0:P, c * TP:(c + 1) * TP], D_xT[s][:, c * P:(c + 1) * P], D_xT[s],
                                  start=True, stop=True)
                    last.then_inc(d_G, 1)
                b = t - 3
                if is_live(b, N):
                    s = (r - 3) % 2
                    pe.wait_ge(d_E, b + 1)
                    wait(pe, d_h, b)
                    for c in range(C):
                        for k in range(C):
                            m = P if k < C - 1 else LAST
                            last = mm(bank[2][0:P, c * (D + 1):(c + 1) * (D + 1)],
                                      D_E[s][0:m, k, c * P:(c + 1) * P], D_x[(r - 3) % 4][0:m, k, :],
                                      start=(k == 0), stop=(k == C - 1))
                    last.then_inc(d_O, 1)
                b = t - 5
                if is_live(b, N):
                    s = (r - 5) % 2
                    pe.wait_ge(d_xT2, b + 1)
                    wait(pe, d_sub, b)
                    for c in range(C):
                        last = mm(bank[4][0:P, c * E:(c + 1) * E], D_xT2[s][:, c * P:(c + 1) * P], wg[:, :],
                                  start=True, stop=True)
                    last.then_inc(d_L, 1)
                b = t - 1
                if is_live(b, N):
                    s = (r - 1) % 2
                    pe.wait_ge(d_x, b + 1)
                    wait(pe, d_xT, b)
                    for c in range(C):
                        last = tr(bank[0][:, c * P:(c + 1) * P], D_x[(r - 1) % 4][:, c, 0:D], ident[0:P, 0:P])
                    last.then_inc(d_T, 1)
                b = t - 4
                if is_live(b, N):
                    s = (r - 4) % 2
                    pe.wait_ge(d_x2, b + 1)
                    wait(pe, d_xT2, b)
                    for c in range(C):
                        last = tr(bank[3][:, c * P:(c + 1) * P], D_x2[s][:, c, :], ident[0:P, 0:P])
                    last.then_inc(d_T2, 1)
            walk(pe, N, LEAD, U, TAIL, phase_d)

            pe.wait_ge(d_S, N)
            for g in range(NG):
                rows_g = min(GB, N - g * GB) * E
                if g >= 2:
                    pe.wait_ge(t_cp, g - 1)
                for c in range(C):
                    last = tr(bank[g % 2][0:rows_g, c * P:(c + 1) * P], gates[:, c, g * 128:g * 128 + rows_g],
                              ident[0:P, 0:P])
                last.then_inc(t_mm, 1)
            for g in range(NG):
                rows_g = min(GB, N - g * GB) * E
                pe.wait_ge(t_id, g + 1)
                if g >= 2:
                    pe.wait_ge(t_slot, g - 1)
                for c in range(C):
                    last = tr(bank[2 + g % 2][0:P, c * 128:c * 128 + rows_g], T_id[g % 2][0:rows_g, c * P:(c + 1) * P],
                              ident[0:rows_g, 0:rows_g])
                last.then_inc(t_mm2, 1)

            def phase_e(t, r):
                if isinstance(t, int) and t == 0:
                    pe.wait_ge(t_slot, NG)
                b = t - 9
                if is_live(b, N):
                    q = ((r - 9) % 8) // 4
                    if r % 4 == 1:
                        pe.wait_ge(e_v, (b + 4) * 2)
                    wait(pe, e_vt, b)
                    for k in range(NB):
                        last = tr(bank[6][0:KB, k * D:(k + 1) * D],
                                  E_vt[q][:, (r - 9) % 4, 2 * k:2 * k + 2, :].rearrange("p e k -> p (e k)"),
                                  ident[:, :])
                    last.then_inc(e_VT, 1)
                q5 = t - 5 - (r - 5) % 4
                live_q = is_live(t - 5, N)
                qs = ((r - 5) % 8) // 4
                e0 = 2 * ((r - 5) % 4)
                u = t - 5

                def up(k):
                    pe.wait_ge(e_xe, q5 + 4)
                    wait(pe, e_hm, 2 * (u * 2 + k) - 2)
                    for f in range(FC):
                        last = mm(bank[3 + k][:, f * Q4 * K:(f + 1) * Q4 * K], w1[:, e0 + k, f * D:(f + 1) * D],
                                  E_xe[qs][:, e0 + k].rearrange("p b k -> p (b k)"), start=True, stop=True)
                    last.then_inc(e_H, 1)

                def down(k):
                    pe.wait_ge(e_hm, 2 * (u * 2 + k) + 2)
                    wait(pe, e_v, u * 2 + k)
                    for f in range(FC):
                        last = mm(bank[5][:, 0:Q4 * K], w2[:, e0 + k, f, :], E_hm[k][:, f, :],
                                  start=(f == 0), stop=(f == FC - 1))
                    last.then_inc(e_V, 1)

                if live_q:
                    up(0)
                b = t - 1
                if is_live(b, N):
                    s = (r - 1) % 2
                    pe.wait_ge(e_x, b + 1)
                    pe.wait_ge(e_P, C * b + 2)
                    wait(pe, e_xe, b)
                    for c in range(C):
                        last = mm(bank[0][:, 0:EK], E_x[s][:, c, :], E_P[s][:, c].rearrange("p e k -> p (e k)"),
                                  start=(c == 0), stop=(c == C - 1))
                    last.then_inc(e_X, 1)
                if live_q:
                    up(1)
                b = t - 9
                if is_live(b, N):
                    pe.wait_ge(e_vt, b + 1)
                    wait(pe, e_o, b)
                    for c in range(C):
                        for k in range(NB):
                            last = mm(bank[7][0:P, c * D:(c + 1) * D], E_PT[(r - 9) % 8][:, c, k, :], E_v[:, k, :],
                                      start=(k == 0), stop=(k == NB - 1))
                    last.then_inc(e_O, 1)
                if live_q:
                    down(0)
                b = t - 1
                if is_live(b, N):
                    for c in range(C):
                        pe.wait_ge(e_PG, C * b + c + 1)
                        wait(pe, e_PTe, C * (b - 1) + c + 1)
                        for k in range(NB):
                            last = tr(bank[1 + c][0:KB, k * P:(k + 1) * P],
                                      E_PG[0][:, c, 2 * k:2 * k + 2, :].rearrange("p e k -> p (e k)"),
                                      ident[0:P, 0:P])
                        last.then_inc(e_PT, 1)
                if live_q:
                    down(1)
            walk(pe, N, LEADE, UE, TAILE, phase_e)

        @block.scalar
        def _(act):
            fn, copy = nc.scalar.activation, nc.scalar.copy

            def phase_a(t, r):
                if isinstance(t, int) and t == 0:
                    act.wait_ge(w_main, 16 * 23)
                b = t - 3
                if is_live(b, N):
                    s = (r - 3) % 2
                    for c in range(C):
                        act.wait_ge(a_sub, 2 * b + c + 1)
                        fn(A_A[s][c], A_A[s][c], ACT.Exp, scale=SCALE).then_inc(a_exp, 1)
                b = t - 1
                if is_live(b, N):
                    s = (r - 1) % 2
                    act.wait_ge(a_T, b + 1)
                    wait(act, a_V, b - 1)
                    fn(A_xT[s], bank[0][:, 0:KV + TP], ACT.Identity, bias=cols[:, 1:2], scale=cols[:, 0:1])\
                        .then_inc(a_xT, 1)
                b = t - 4
                if is_live(b, N):
                    s = (r - 4) % 2
                    for c in range(C):
                        act.wait_ge(a_AT, 2 * b + c + 1)
                        wait(act, a_AV, b - 1)
                        copy(A_AT[s][:, c].rearrange("p h k -> p (h k)"), bank[7 if c == 0 else 1][:, 0:H * P])\
                            .then_inc(a_ATe, 1)
                b = t - 2
                if is_live(b, N):
                    act.wait_ge(a_V, b + 1)
                    wait(act, a_AV, b - 3)
                    copy(A_V[(r - 2) % 4].rearrange("p h d -> p (h d)"), bank[4][:, :]).then_inc(a_Ve, 1)
            walk(act, N, LEAD, U, TAIL, phase_a)

            def phase_b(t, r):
                if isinstance(t, int) and t == 0:
                    act.wait_ge(a_y, N)
                b = t - 1
                if is_live(b, N):
                    s = (r - 1) % 2
                    act.wait_ge(b_T, b + 1)
                    wait(act, b_H, b - 1)
                    fn(B_ynT[s], bank[0][:, 0:TP], ACT.Identity, bias=cols[:, 3:4], scale=cols[:, 2:3])\
                        .then_inc(b_ynT, 1)
                b = t - 3
                if is_live(b, N):
                    s = (r - 3) % 2
                    act.wait_ge(b_T2, b + 1)
                    wait(act, b_Q, b - 1)
                    copy(B_xT[s], bank[2][:, 0:TP]).then_inc(b_xT, 1)
                b = t - 5
                if is_live(b, N):
                    s = (r - 5) % 2
                    act.wait_ge(b_F, b + 1)
                    copy(spectra[:, b].rearrange("p r d -> p (r d)"), bank[4][0:NF, 0:2 * D])
                    wait(act, b_P, b - 1)
                    wait(act, b_pw, b)
                    fn(B_junk, bank[4][0:NF, 0:2 * D], ACT.Square, accum_out=B_pw[s]).then_inc(b_pw, 1)
            walk(act, N, LEAD, U, TAIL, phase_b)

            def phase_c(t, r):
                if isinstance(t, int) and t == 0:
                    act.wait_ge(k_cp, 7)
                if is_live(t, N):
                    s = r % 2
                    wait(act, c_I, t - 1)
                    factor = wfreq[:, t:t + 1] if isinstance(t, int) else wfreq[:, bass.ds(t, 1)]
                    fn(C_G[s], spectra[:, t], ACT.Copy, scale=factor).then_inc(c_G, 1)
                b = t - 4
                if is_live(b, N):
                    s = (r - 4) % 2
                    act.wait_ge(c_CT, b + 1)
                    wait(act, c_B, b - 1)
                    copy(C_cT[s], bank[7][0:C * E, 0:P]).then_inc(c_cT, 1)
                b = t - 4
                if is_live(b, N):
                    s = (r - 4) % 2
                    wait(act, c_add1, b)
                    for c in range(C):
                        act.wait_ge(c_E, 4 * b + 2 * c + 2)
                        for e in range(E // 2):
                            last = fn(C_t[:, c, e, :], bank[4 + 2 * c][0:P, e * D:(e + 1) * D], ACT.Copy,
                                      scale=C_c[s][:, c, E // 2 + e:E // 2 + e + 1])
                        last.then_inc(c_act, 1)
                b = t - 2
                if is_live(b, N):
                    act.wait_ge(c_T, b + 1)
                    wait(act, c_E, 4 * (b - 3))
                    copy(C_xT[(r - 2) % 4], bank[1][:, 0:TP]).then_inc(c_xT, 1)
                b = t - 3
                if is_live(b, N):
                    s = (r - 3) % 2
                    act.wait_ge(c_sub, b + 1)
                    fn(C_ex[s], C_ex[s], ACT.Exp).then_inc(c_exp, 1)
            walk(act, N, LEAD, U, TAIL, phase_c)

            def phase_d(t, r):
                if isinstance(t, int) and t == 0:
                    act.wait_ge(c_out, N)
                b = t - 2
                if is_live(b, N):
                    s = (r - 2) % 2
                    act.wait_ge(d_G, b + 1)
                    wait(act, d_O, b - 1)
                    fn(D_E[s].rearrange("p c k -> p (c k)"), bank[1][0:P, 0:C * TP], ACT.Exp,
                       bias=mshift[0:P, :]).then_inc(d_E, 1)
                b = t - 1
                if is_live(b, N):
                    s = (r - 1) % 2
                    act.wait_ge(d_T, b + 1)
                    wait(act, d_G, b - 1)
                    copy(D_xT[s], bank[0][:, 0:TP]).then_inc(d_xT, 1)
                b = t - 4
                if is_live(b, N):
                    s = (r - 4) % 2
                    act.wait_ge(d_T2, b + 1)
                    wait(act, d_L, b - 1)
                    copy(D_xT2[s], bank[3][:, 0:TP]).then_inc(d_xT2, 1)
                b = t - 5
                if is_live(b, N):
                    s = (r - 5) % 2
                    act.wait_ge(d_sub, b + 1)
                    fn(D_lg[s], D_lg[s], ACT.Exp).then_inc(d_exp, 1)
            walk(act, N, LEAD, U, TAIL, phase_d)

            def phase_e(t, r):
                if isinstance(t, int) and t == 0:
                    act.wait_ge(t_slot, NG)
                u = t - 5
                e0 = 2 * ((r - 5) % 4)

                def gelu(k):
                    act.wait_ge(e_H, u * 2 + k + 1)
                    wait(act, e_V, u * 2 + k - 1)
                    for f in range(FC):
                        fn(E_hm[k][:, f, :], bank[3 + k][:, f * Q4 * K:(f + 1) * Q4 * K], ACT.Gelu,
                           bias=b1col[:, e0 + k, f:f + 1], scale=1.0).then_inc(e_hm, 1)

                if is_live(u, N):
                    gelu(0)
                b = t - 1
                if is_live(b, N):
                    q = ((r - 1) % 8) // 4
                    act.wait_ge(e_X, b + 1)
                    if (r - 1) % 4 == 0:
                        wait(act, e_H, 2 * (b - 4))
                    copy(E_xe[q][:, :, (r - 1) % 4, :], bank[0][:, 0:EK].rearrange("p (e k) -> p e k", e=E))\
                        .then_inc(e_xe, 1)
                if is_live(u, N):
                    gelu(1)
                if is_live(b, N):
                    wait(act, e_O, b - 7)
                    for c in range(C):
                        act.wait_ge(e_PT, C * b + c + 1)
                        copy(E_PT[(r - 1) % 8][:, c].rearrange("p n k -> p (n k)"), bank[1 + c][0:KB, 0:NB * P])\
                            .then_inc(e_PTe, 1)
            walk(act, N, LEADE, UE, TAILE, phase_e)

        @block.vector
        def _(dve):
            v = nc.vector

            dve.wait_ge(w_prep, 16 * 10)
            dve.wait_ge(c_set, 3)
            v.tensor_copy(bvwide, bvcol.unsqueeze(2).broadcast_to([D, H, P])).then_inc(p_cp, 1)
            dve.wait_ge(p_mm, 1)
            v.tensor_copy(wvT, bank[0][:, 0:H * D].rearrange("p (h d) -> p h d", h=H)).then_inc(p_cp, 1)
            dve.wait_ge(p_mm, 2)
            for c in range(C):
                v.tensor_copy(gamT[:, c, :], bank[2][:, 0:E])
            v.tensor_copy(insmean, bank[1][:, 0:1]).then_inc(p_cp, 1)
            dve.wait_ge(p_cp, 3)
            v.tensor_copy(inswide, insmean.broadcast_to([D, D]))
            CE = C * E
            v.tensor_copy(inssel[:, 0:(CE - 1) * (CE + 1) + 1:CE + 1], insmean.broadcast_to([D, CE])).then_inc(p_cp, 1)
            dve.wait_ge(p_mm, 3)
            dve.wait_ge(c_set, 4)
            v.tensor_tensor(crow[:, :], bank[3][0:P, 0:D], b1row, ALU.add).then_inc(p_cp, 1)
            v.tensor_copy(wvo[:, :, :].rearrange("p h d -> p (h d)"), bank[4][:, 0:H * D]).then_inc(p_cp, 1)
            dve.wait_ge(p_mm, 4)
            v.tensor_copy(rgrow[:, :], bank[5][0:P, 0:E])
            v.tensor_copy(gamcol, bank[5][0:CE, 16:17]).then_inc(p_cp, 1)
            v.tensor_copy(gamrow, bank[6][:, 0:E]).then_inc(p_cp, 1)
            dve.wait_ge(p_cp, 8)
            v.tensor_tensor(wx[:, :, :], wx[:, :, :], gamrow.unsqueeze(2).broadcast_to([D, E, D]), ALU.mult)\
                .then_inc(p_cp, 1)
            dve.wait_ge(w_eb, 32)
            v.scalar_tensor_tensor(out=bmod[:, :, :].rearrange("p c d -> p (c d)"),
                                   in0=ebz.rearrange("p c d -> p (c d)"), scalar=gamcol,
                                   in1=bank[7][0:CE, 0:C * D], op0=ALU.mult, op1=ALU.add).then_inc(p_cp, 1)

            def stats(b, src, st, mv, s_bn, s_mv):
                for c in range(len(src)):
                    m = src[c].shape[0]
                    last = v.bn_stats(st[0:m, c, :], src[c])
                last.then_inc(s_bn, 1)
                wait_apart(dve, s_bn, b + 1, c_set)
                for c in range(len(src)):
                    m = src[c].shape[0]
                    last = v.bn_aggr(mv[0:m, c, :], st[0:m, c, :])
                last.then_inc(s_mv, 1)

            def normalise(b, src, dst, mv, rstd, s_rstd, s_x):
                dve.wait_ge(s_rstd, b + 1)
                for c in range(len(src)):
                    m = src[c].shape[0]
                    last = v.tensor_scalar(dst[c], src[c], mv[0:m, c, 0:1], rstd[0:m, c:c + 1],
                                           ALU.subtract, ALU.mult)
                last.then_inc(s_x, 1)

            def chunks(ap):
                return [ap[:, c, :] for c in range(C)]

            def phase_a(t, r):
                if isinstance(t, int) and t == 0:
                    dve.wait_ge(w_main, 16 * 23)
                if is_live(t, N):
                    s = r % 2
                    src = [A_xk[s]] + chunks(A_xq[s])
                    wait_apart(dve, a_in[s], dma_count(t, s, 2, 16 * (C + 1)), c_set)
                    stats(t, src, A_st[s], A_mv[s], a_bn, a_mv)
                b = t - 2
                if is_live(b, N):
                    s = (r - 2) % 2
                    for i in range(2):
                        dve.wait_ge(a_Q, 2 * b + i + 1)
                        wait(dve, a_S, 2 * (b - 1))
                        v.tensor_tensor(A_QT[s][:, 2 * i:2 * i + 2, :],
                                        bank[1 + i][:, 0:2 * TP].rearrange("p (h k) -> p h k", h=2),
                                        cols[:, 4 + 2 * i:6 + 2 * i].unsqueeze(2).broadcast_to([D, 2, TP]),
                                        ALU.add).then_inc(a_Qe, 1)
                b = t - 3
                if is_live(b, N):
                    s = (r - 3) % 2
                    score = [bank[5 + c][0:P, :].rearrange("p (h k) -> p h k", h=H) for c in range(C)]
                    for c in range(C):
                        dve.wait_ge(a_S, 2 * b + c + 1)
                        v.tensor_reduce(A_mx[s][:, c, :], score[c], AX.X, ALU.max).then_inc(a_mx, 1)
                    for c in range(C):
                        dve.wait_ge(a_mx, 2 * b + c + 1)
                        wait(dve, a_AT, 2 * b + c - 3)
                        v.tensor_tensor(A_A[s][c], score[c], A_mx[s][:, c, :].unsqueeze(2).broadcast_to([P, H, KV]),
                                        ALU.subtract).then_inc(a_sub, 1)
                if is_live(t, N):
                    s = r % 2
                    wait(dve, a_T, t - 1)
                    wait(dve, a_res, t - 1)
                    normalise(t, src, [A_xn[s][:, 0, :], A_xn[s][0:P, 1, :], A_xn[s][0:P, 2, :]],
                              A_mv[s], A_rstd[s], a_rstd, a_xn)
                b = t - 3
                if is_live(b, N):
                    for c in range(C):
                        dve.wait_ge(a_exp, 2 * b + c + 1)
                        v.tensor_reduce(A_sm[s_(r, 3)][:, c, :], A_A[s_(r, 3)][c], AX.X, ALU.add).then_inc(a_sum, 1)
                    dve.wait_ge(a_sum, 2 * b + 2)
                    wait(dve, a_An, 2 * (b - 1))
                    v.reciprocal(A_rc[s_(r, 3)], A_sm[s_(r, 3)]).then_inc(a_rcp, 1)
                b = t - 5
                if is_live(b, N):
                    dve.wait_ge(a_AV, b + 1)
                    dve.wait_ge(a_res, b + 1)
                    v.tensor_tensor(h[:, b], bank[2][0:P, 0:C * D].rearrange("p (c d) -> p c d", c=C), h[:, b],
                                    ALU.add).then_inc(a_y, 1)
                b = t - 2
                if is_live(b, N):
                    s = (r - 2) % 2
                    dve.wait_ge(a_K, b + 1)
                    wait(dve, a_S, 2 * (b - 1))
                    v.tensor_tensor(A_KT[s], bank[3][:, :].rearrange("p (h k) -> p h k", h=H),
                                    cols[:, 4 + H:4 + 2 * H].unsqueeze(2).broadcast_to([D, H, KV]),
                                    ALU.add).then_inc(a_Ke, 1)

            def s_(r, k):
                return (r - k) % 2
            walk(dve, N, LEAD, U, TAIL, phase_a)

            def phase_b(t, r):
                if isinstance(t, int) and t == 0:
                    dve.wait_ge(a_y, N)
                b = t - 1
                if is_live(b, N):
                    s = (r - 1) % 2
                    wait(dve, b_T, b - 1)
                    normalise(b, chunks(h[:, b]), chunks(B_yn[s]), B_mv[s], B_rstd[s], b_rstd, b_yn)
                b = t - 3
                if is_live(b, N):
                    s = (r - 3) % 2
                    wait(dve, b_T2, b - 1)
                    wait(dve, b_res, b - 1)
                    normalise(b, chunks(B_h[s]), chunks(B_x[s]), B_mv2[s], B_rstd2[s], b_rstd2, b_x)
                if is_live(t, N):
                    s = r % 2
                    stats(t, chunks(h[:, t]), B_st[s], B_mv[s], b_bn, b_mv)
                b = t - 2
                if is_live(b, N):
                    s = (r - 2) % 2
                    dve.wait_ge(b_H, b + 1)
                    wait(dve, b_res, b - 1)
                    v.tensor_tensor(B_h[s], bank[1][0:P, 0:C * D].rearrange("p (c d) -> p c d", c=C),
                                    bfrow[:, :].unsqueeze(1).broadcast_to([P, C, D]), ALU.add).then_inc(b_h, 1)
                    wait_apart(dve, b_h, b + 1, c_set)
                    stats(b, chunks(B_h[s]), B_st2[s], B_mv2[s], b_bn2, b_mv2)
                b = t - 4
                if is_live(b, N):
                    s = (r - 4) % 2
                    dve.wait_ge(b_Q, b + 1)
                    wait(dve, b_F, b - 1)
                    v.tensor_tensor(B_q[s], bank[3][0:P, 0:C * D].rearrange("p (c d) -> p c d", c=C),
                                    barow[:, :].unsqueeze(1).broadcast_to([P, C, D]), ALU.add).then_inc(b_q, 1)
            walk(dve, N, LEAD, U, TAIL, phase_b)

            ND = NF - 1
            dve.wait_ge(k_mm, 1)
            dve.wait_ge(b_P, N)
            v.memset(K_sel, LOWEST)
            v.memset(K_cr, LOWEST)
            v.memset(K_w, 1.0 / DELAYS).then_inc(k_cp, 1)
            dve.wait_ge(k_cp, 1)
            v.tensor_copy(K_cr[:, 0:ND], bank[5][0:N, 1:NF]).then_inc(k_cp, 1)
            dve.wait_ge(k_cp, 2)
            v.max(K_m8, K_cr).then_inc(k_cp, 1)
            dve.wait_ge(k_cp, 3)
            v.tensor_copy(K_sel[:, 0:PAIRS], K_m8[:, 0:PAIRS]).then_inc(k_cp, 1)
            dve.wait_ge(k_cp, 4)
            v.match_replace(K_mr, K_sel, K_cr, TAKEN).then_inc(k_own, 1)
            dve.wait_ge(k_own, 1)
            v.tensor_scalar(K_w[:, 1:NF], K_mr[:, 0:ND], TAKEN, 2.0 / DELAYS, ALU.is_equal, ALU.mult).then_inc(k_cp, 1)
            dve.wait_ge(k_mm, 2)
            v.tensor_copy(K_wT, bank[6][0:NF, 0:N]).then_inc(k_cp, 1)
            dve.wait_ge(k_mm, 3)
            v.tensor_copy(wfreq[:, :], bank[7][0:NF, 0:N]).then_inc(k_cp, 1)

            for s in range(2):
                v.memset(C_lg[s], LOWEST)
                v.memset(C_sel[s], LOWEST).then_inc(c_set2, 1)
            dve.wait_ge(c_set2, 2)
            dve.wait_ge(b_res, N)

            def phase_c(t, r):
                b = t - 2
                if is_live(b, N):
                    s = (r - 2) % 2
                    wait(dve, c_T, b - 1)
                    normalise(b, chunks(C_h[(r - 2) % 4]), chunks(C_x[s]), C_mv[s], C_rstd[s], c_rstd, c_x)
                b = t - 4
                if is_live(b, N):
                    s = (r - 4) % 2
                    dve.wait_ge(c_exp, b + 1)
                    dve.wait_ge(c_mr, b + 1)
                    v.tensor_reduce(C_sm[s], C_ex[s], AX.X, ALU.add).then_inc(c_sum, 1)
                    dve.wait_ge(c_sum, b + 1)
                    v.scalar_tensor_tensor(out=C_ex[s], in0=C_mr[s][:, :, 0:E], scalar=TAKEN, in1=C_ex[s],
                                           op0=ALU.is_equal, op1=ALU.mult).then_inc(c_cu, 1)
                    v.reciprocal(C_rc[s], C_sm[s]).then_inc(c_rcp, 1)
                    dve.wait_ge(c_rcp, b + 1)
                    dve.wait_ge(c_cu, b + 1)
                    wait(dve, c_CT, b - 1)
                    wait(dve, c_act, C * (b - 1))
                    v.tensor_tensor(C_c[s], C_ex[s], C_rc[s].unsqueeze(2).broadcast_to([P, C, E]), ALU.mult)\
                        .then_inc(c_c, 1)
                b = t - 5
                if is_live(b, N):
                    dve.wait_ge(c_add2, b + 1)
                    dve.wait_ge(c_stt, E * (b + 1))
                    v.tensor_tensor(h[:, b], C_h[(r - 5) % 4], C_u[:, :, 0, :], ALU.add).then_inc(c_out, 1)
                b = t - 1
                if is_live(b, N):
                    s = (r - 1) % 2
                    dve.wait_ge(c_I, b + 1)
                    wait(dve, c_out, b - 3)
                    v.tensor_tensor(C_h[(r - 1) % 4], bank[0][0:P, 0:C * D].rearrange("p (c d) -> p c d", c=C),
                                    h[:, b], ALU.add).then_inc(c_h, 1)
                    wait_apart(dve, c_h, b + 1, c_set)
                    stats(b, chunks(C_h[(r - 1) % 4]), C_st[s], C_mv[s], c_bn, c_mv)
                b = t - 3
                if is_live(b, N):
                    s = (r - 3) % 2
                    dve.wait_ge(c_L, b + 1)
                    v.tensor_tensor(C_lg[s][:, :, 0:E], bank[2][0:P, 0:C * E].rearrange("p (c e) -> p c e", c=C),
                                    rgrow[:, :].unsqueeze(1).broadcast_to([P, C, E]), ALU.add).then_inc(c_lg, 1)
                    wait_apart(dve, c_lg, b + 1, c_set)
                    for c in range(C):
                        last = v.max(C_m8[s][:, c, :], C_lg[s][:, c, 0:E])
                    last.then_inc(c_m8, 1)
                    dve.wait_ge(c_m8, b + 1)
                    v.tensor_tensor(C_ex[s], C_lg[s][:, :, 0:E], C_m8[s][:, :, 0:1].broadcast_to([P, C, E]),
                                    ALU.subtract).then_inc(c_sub, 1)
                    v.tensor_copy(C_sel[s][:, :, 0:2], C_m8[s][:, :, 0:2]).then_inc(c_sel, 1)
                    wait_apart(dve, c_sel, b + 1, c_set)
                    for c in range(C):
                        last = v.match_replace(C_mr[s][:, c, :], C_sel[s][:, c, :], C_lg[s][:, c, :], TAKEN)
                    last.then_inc(c_mr, 1)
                b = t - 4
                if is_live(b, N):
                    s = (r - 4) % 2
                    acc = C_h[(r - 4) % 4]
                    dve.wait_ge(c_B, b + 1)
                    v.tensor_tensor(acc, bank[7][0:P, 128:128 + C * D].rearrange("p (c d) -> p c d", c=C), acc,
                                    ALU.add).then_inc(c_hb, 1)
                    dve.wait_ge(c_hb, b + 1)
                    for e in range(E // 2):
                        for c in range(C):
                            if e == 0:
                                dve.wait_ge(c_E, 4 * b + 2 * c + 1)
                            else:
                                dve.wait_ge(c_stt, E * b + 2 * e + c - 1)
                            v.scalar_tensor_tensor(out=acc[:, c, :], in0=bank[3 + 2 * c][0:P, e * D:(e + 1) * D],
                                                   scalar=C_c[s][:, c, e:e + 1], in1=acc[:, c, :],
                                                   op0=ALU.mult, op1=ALU.add).then_inc(c_stt, 1)
            walk(dve, N, LEAD, U, TAIL, phase_c)

            dve.wait_ge(c_out, N)
            for s in range(4):
                last = v.memset(D_x[s][:, :, D:D + 1], 1.0)
            last.then_inc(c_set2, 1)
            dve.wait_ge(c_set2, 3)

            def phase_d(t, r):
                b = t - 1
                if is_live(b, N):
                    s = (r - 1) % 2
                    wait(dve, d_T, b - 3)
                    wait(dve, d_O, b - 3)
                    normalise(b, chunks(h[:, b]), [D_x[(r - 1) % 4][:, c, 0:D] for c in range(C)], D_mv[s], D_rstd[s],
                              d_rstd, d_x)
                b = t - 4
                if is_live(b, N):
                    s = (r - 4) % 2
                    wait(dve, d_T2, b - 1)
                    normalise(b, chunks(h[:, b]), chunks(D_x2[s]), D_mv2[s], D_rstd2[s], d_rstd2, d_x2)
                b = t - 6
                if is_live(b, N):
                    s = (r - 6) % 2
                    dve.wait_ge(d_exp, b + 1)
                    v.tensor_reduce(D_sm[s], D_lg[s], AX.X, ALU.add).then_inc(d_sum, 1)
                    dve.wait_ge(d_sum, b + 1)
                    v.reciprocal(D_rc2[s], D_sm[s]).then_inc(d_rcp2, 1)
                    dve.wait_ge(d_rcp2, b + 1)
                    dst = gates[:, :, E * b:E * b + E] if isinstance(b, int) else gates[:, :, bass.ds(b * E, E)]
                    v.tensor_tensor(dst, D_lg[s], D_rc2[s].unsqueeze(2).broadcast_to([P, C, E]), ALU.mult)\
                        .then_inc(d_S, 1)
                if is_live(t, N):
                    s = r % 2
                    stats(t, chunks(h[:, t]), D_st[s], D_mv[s], d_bn, d_mv)
                b = t - 3
                if is_live(b, N):
                    s = (r - 3) % 2
                    o = bank[2][0:P, 0:C * (D + 1)].rearrange("p (c d) -> p c d", c=C)
                    dve.wait_ge(d_O, b + 1)
                    v.reciprocal(D_rc[s], o[:, :, D]).then_inc(d_rcp, 1)
                    dve.wait_ge(d_rcp, b + 1)
                    for c in range(C):
                        last = v.scalar_tensor_tensor(out=h[:, b, c, :], in0=o[:, c, 0:D], scalar=D_rc[s][:, c:c + 1],
                                                      in1=h[:, b, c, :], op0=ALU.mult, op1=ALU.add)
                    last.then_inc(d_h, 1)
                    wait_apart(dve, d_h, b + 1, c_set)
                    stats(b, chunks(h[:, b]), D_st2[s], D_mv2[s], d_bn2, d_mv2)
                b = t - 5
                if is_live(b, N):
                    s = (r - 5) % 2
                    lg = bank[4][0:P, 0:C * E].rearrange("p (c e) -> p c e", c=C)
                    dve.wait_ge(d_L, b + 1)
                    v.tensor_reduce(D_mx[s], lg, AX.X, ALU.max).then_inc(d_mx, 1)
                    dve.wait_ge(d_mx, b + 1)
                    v.tensor_tensor(D_lg[s], lg, D_mx[s].unsqueeze(2).broadcast_to([P, C, E]),
                                    ALU.subtract).then_inc(d_sub, 1)
            walk(dve, N, LEAD, U, TAIL, phase_d)

            dve.wait_ge(d_S, N)
            dve.wait_ge(d_T2, N)
            v.memset(T_one, 1.0)
            for s in range(2):
                v.memset(T_id[s], -1.0)
                v.memset(T_s[s], LOWEST).then_inc(t_set, 1)
            dve.wait_ge(t_set, 2)

            def slots_out(g):
                n = min(GB, N - g * GB) * E
                dve.wait_ge(t_mm2, g + 1)
                v.tensor_copy(slots[:, :, g * 128:g * 128 + n],
                              bank[2 + g % 2][0:P, 0:C * 128].rearrange("p (c k) -> p c k", c=C)[:, :, 0:n])\
                    .then_inc(t_slot, 1)
            rounds = (K + 7) // 8
            short = K - 8 * (rounds - 1)
            assert 8 - short <= 3
            for g in range(NG):
                s = g % 2
                n = min(GB, N - g * GB) * E
                dve.wait_ge(t_mm, g + 1)
                v.tensor_copy(T_s[s][0:n, 0:T], bank[g % 2][0:n, 0:T]).then_inc(t_cp, 1)
                dve.wait_ge(t_cp, g + 1)
                for k in range(rounds):
                    at = g * rounds + k
                    src = T_s[s] if k == 0 else T_w[s]
                    v.max(T_m8[s][0:n], src[0:n, 0:T]).then_inc(t_top, 1)
                    dve.wait_ge(t_top, g * (rounds + 1) + k + 1)
                    if k == rounds - 1 and short < 8:
                        v.memset(T_m8[s][0:n, short:], LOWEST).then_inc(t_top, 1)
                        dve.wait_ge(t_top, (g + 1) * (rounds + 1))
                    v.match_replace(T_w[s][0:n], T_m8[s][0:n], src[0:n], CHOSEN)\
                        .then_inc(t_mr, 1)
                    dve.wait_ge(t_mr, at + 1)
                v.tensor_scalar(T_w[s][0:n, 0:T], T_w[s][0:n, 0:T], CHOSEN, None, ALU.is_equal).then_inc(t_mask, 1)
                dve.wait_ge(t_mask, g + 1)
                v.tensor_tensor_scan(T_pos[s][0:n], T_one[0:n], T_w[s][0:n, 0:T], 0.0, ALU.mult, ALU.add)\
                    .then_inc(t_scan, 1)
                dve.wait_ge(t_scan, g + 1)
                v.tensor_tensor(T_pos[s][0:n], T_pos[s][0:n], T_w[s][0:n, 0:T], ALU.mult).then_inc(t_id0, 1)
                dve.wait_ge(t_id0, g + 1)
                wait(dve, t_mm2, g - 1)
                v.tensor_scalar(T_id[s][0:n, 0:T], T_pos[s][0:n], -1.0, None, ALU.add).then_inc(t_id, 1)
                if g >= 1:
                    slots_out(g - 1)
            slots_out(NG - 1)

            def phase_e(t, r):
                if is_live(t, N):
                    s = r % 2
                    if isinstance(t, int) and t == 0:
                        dve.wait_ge(t_slot, NG)
                    stats(t, chunks(h[:, t]), E_st[s], E_mv[s], e_bn, e_mv)
                b = t - 9
                if is_live(b, N):
                    dve.wait_ge(e_VT, b + 1)
                    wait(dve, e_O, b)
                    v.tensor_copy(E_v.rearrange("p n d -> p (n d)"), bank[6][0:KB, 0:NB * D]).then_inc(e_vt, 1)
                if is_live(t, N):
                    s = r % 2
                    for c in range(C):
                        wait(dve, e_X, t - 1)
                        wait(dve, e_PG, C * (t - 1))
                        no = slots[:, c, E * t:E * t + E] if isinstance(t, int) else slots[:, c, bass.ds(t * E, E)]
                        v.tensor_tensor(E_P[s][:, c], slotno[:, :].unsqueeze(1).broadcast_to([P, E, K]),
                                        no.unsqueeze(2).broadcast_to([P, E, K]), ALU.is_equal).then_inc(e_P, 1)
                    normalise(t, chunks(h[:, t]), chunks(E_x[s]), E_mv[s], E_rstd[s], e_rstd, e_x)
                u = t - 5
                e0 = 2 * ((r - 5) % 4)
                qs = ((r - 5) % 8) // 4

                def down(k):
                    dve.wait_ge(e_V, u * 2 + k + 1)
                    if (r - 5) % 4 == 0 and k == 0:
                        wait(dve, e_VT, u - 4)
                    v.tensor_scalar(E_vt[qs][:, :, e0 + k, :], bank[5][:, 0:Q4 * K].rearrange("p (b k) -> p b k", b=Q4),
                                    b2col[:, e0 + k:e0 + k + 1], None, ALU.add).then_inc(e_v, 1)

                if is_live(u, N):
                    down(0)
                b = t - 9
                if is_live(b, N):
                    dve.wait_ge(e_O, b + 1)
                    v.tensor_tensor(h[:, b], bank[7][0:P, 0:C * D].rearrange("p (c d) -> p c d", c=C), h[:, b],
                                    ALU.add).then_inc(e_o, 1)
                if is_live(u, N):
                    down(1)
            walk(dve, N, LEADE, UE, TAILE, phase_e)


_INS = ['L0_tok_g1', 'L0_tok_b1', 'L0_tok_Wq', 'L0_tok_bq', 'L0_tok_Wk', 'L0_tok_bk', 'L0_tok_Wv', 'L0_tok_bv',
        'L0_tok_Wo', 'L0_tok_bo', 'L0_tok_g2', 'L0_tok_b2', 'L0_tok_Wf', 'L0_tok_bf', 'L0_attn_W', 'L0_attn_b',
        'L0_ffn_Ins_tk', 'L0_ffn_gate_w', 'L0_ffn_expert_w', 'L0_ffn_expert_b', 'L0_ffn_gamma_w', 'L0_ffn_beta_w',
        'L0_ffn_rmod_w', 'L1_ffn_Wg', 'L1_ffn_W1', 'L1_ffn_b1', 'L1_ffn_W2', 'L1_ffn_b2']


def _fourier_tables(T):
    import numpy as np
    half = T // 2 + 1
    angle = 2.0 * np.pi * (np.outer(np.arange(T), np.arange(half)) % T) / T
    weight = np.full(half, 2.0 / T)
    weight[0] = 1.0 / T
    forward, inverse = [], []
    for f in (np.cos, np.sin):
        table = np.zeros((2 * half, half))
        table[:T] = f(angle)
        forward.append(table.astype(np.float32))
        inverse.append(np.ascontiguousarray((table * weight).T.astype(np.float32)))
    return forward + inverse


def kernel(**inputs):
    import numpy as _np
    import concourse.bacc as _bacc
    from concourse import mybir as _mybir
    from concourse.bass_utils import run_bass_kernel_spmd as _run

    nc = _bacc.Bacc("TRN2", target_bir_lowering=False, num_devices=1)
    x = _np.ascontiguousarray(inputs["x"])
    arrays, args = {}, []

    def give(name, a):
        arrays[name] = a
        args.append(nc.dram_tensor(name, a.shape, _mybir.dt.from_np(a.dtype), kind="ExternalInput").ap())

    n, s, d = x.shape
    t = s - 128
    give("in_x_dram", x)
    for name, table in zip(("fwd_cos", "fwd_sin", "inv_cos", "inv_sin"), _fourier_tables(t)):
        give(f"table_{name}_dram", table)
    for name in _INS:
        give(f"in_{name}_dram", _np.ascontiguousarray(inputs[name]))
    result = nc.dram_tensor("out_0_dram", (n, t, d), _mybir.dt.float32, kind="ExternalOutput").ap()
    audio_tower(nc, *args, result)
    r = _run(nc, [arrays], core_ids=[0])
    return r.results[0]["out_0_dram"]
```

```python
from contextlib import ExitStack

import concourse.bass as bass
from concourse import mybir

F32 = mybir.dt.float32
F32R = mybir.dt.float32r
ALU = mybir.AluOpType
ACT = mybir.ActivationFunctionType
AX = mybir.AxisListType

EPS = 1e-5
LOWEST = -3e38
TAKEN = 3e38
CHOSEN = -2e38
SHIFT = 64.0


def is_live(b, n):
    return not isinstance(b, int) or 0 <= b < n


def wait(eng, sem, value):
    if not isinstance(value, int) or value > 0:
        eng.wait_ge(sem, value)


def wait_apart(eng, sem, value, met):
    if isinstance(value, int):
        eng.wait_ge(sem, value)
    else:
        register = eng.to_reg(value)
        eng.wait_ge(met, 1)
        eng.wait_ge(sem, register)


def dma_count(b, slot, slots, per):
    if isinstance(b, int):
        return (b // slots + 1) * per
    return (b - slot) * (per // slots) + per


def walk(eng, n, lead, unroll, tail, step):
    assert lead % unroll == 0 and (n - lead) % unroll == 0 and n > lead
    for t in range(lead):
        step(t, t % unroll)
    with eng.Fori(lead, n - unroll + 1, unroll) as t:
        for r in range(unroll):
            step(t + r, r)
    for t in range(n, n + tail):
        step(t, t % unroll)


def audio_tower(nc, x, tab_fwd_cos, tab_fwd_sin, tab_inv_cos, tab_inv_sin,
                g1, b1, Wq, bq, Wk, bk, Wv, bv, Wo, bo, g2, b2, Wf, bf,
                Wa, ba, ins, gate_w, expert_w, expert_b, gamma_w, beta_w, rmod_w,
                Wg, W1, eb1, W2, eb2, out):
    N, S, D = x.shape
    H = Wq.shape[0]
    T = out.shape[1]
    KV = S - T
    C = 2
    P = (T + C - 1) // C
    TP = C * P
    LAST = T - P
    NI = ins.shape[1]
    E = gate_w.shape[1]
    F = W1.shape[2]
    FC = F // D
    K = min(max(T * 2 // E, 1), T)
    DELAYS = 1
    while 2 ** (DELAYS + 1) <= T:
        DELAYS += 1
    NF = T // 2 + 1
    PAIRS = (DELAYS - 1) // 2
    assert D == 128 and KV == 128 and T % 2 == 1 and DELAYS % 2 == 1 and NF == P and N <= 128
    assert E == 8
    SCALE = float(D) ** -0.5
    EK = E * K
    NB = 4
    KB = EK // NB
    Q4 = 4
    U, LEAD, TAIL = 4, 8, 6
    UE, LEADE, TAILE = 8, 16, 9

    with ExitStack() as ctx:
        def sb(name, shape, dt=F32):
            return ctx.enter_context(nc.sbuf_tensor(name, shape, dt))

        def sem(name):
            return ctx.enter_context(nc.semaphore(name))

        bank = [ctx.enter_context(nc.psum_tensor(f"bank{i}", [128, 512], F32)) for i in range(8)]

        with ExitStack() as weights:
            def early(name, shape):
                return weights.enter_context(nc.sbuf_tensor(name, shape, F32))
            wq = early("wq", [D, H, D])
            wk = early("wk", [D, H, D])
            wvo = early("wvo", [D, H, D])
            wx = early("wx", [D, E, D])
            inv = early("inv", [NF, 2, TP])
        E_P = [sb(f"E_P{s}", [P, C, E, K], F32R) for s in range(2)]
        E_xh = [sb(f"E_xh{s}", [P, C, D], F32R) for s in range(2)]
        E_xl = [sb(f"E_xl{s}", [P, C, D], F32R) for s in range(2)]
        sb("rest", [128, 3 * H * D + E * D + 2 * TP - 2 * C * E * K - 4 * C * D])

        h = sb("h", [P, N, C, D])
        wide = sb("wide", [128, 64 * 256])
        narrow = sb("narrow", [128, 5600])
        ident = sb("ident", [128, 128])
        fwd = sb("fwd", [P, 2, C, NF])
        wf = sb("wf", [D, D])
        wa = sb("wa", [D, D])
        gatew = sb("gatew", [D, E])
        wg = sb("wg", [D, E])
        w1 = sb("w1", [D, E, F])
        w2 = sb("w2", [D, E, FC, D])
        cols = sb("cols", [D, 4 + 2 * H])
        b1col = sb("b1col", [D, E, FC])
        b2col = sb("b2col", [D, E])
        g1row = sb("g1row", [P, D])
        bfrow = sb("bfrow", [P, D])
        barow = sb("barow", [P, D])
        crow = sb("crow", [P, D])
        rgrow = sb("rgrow", [P, E])
        bmod = sb("bmod", [C * E, C, D])
        slotno = sb("slotno", [P, K])
        mhalf = sb("mhalf", [128, 4])
        epsilon = sb("epsilon", [128, 4])
        nought = sb("nought", [128, 4])
        mshift = sb("mshift", [128, 1])
        power = sb("power", [NF, N])
        wfreq = sb("wfreq", [NF, N])
        gates = sb("gates", [P, C, N * E])
        slots = sb("slots", [P, C, N * E])

        taken = {}

        def carve(tensor, start=0):
            taken[0] = start

            def piece(parts, *shape):
                size = 1
                for s in shape:
                    size *= s
                at = taken[0]
                taken[0] = at + size
                assert at + size <= tensor.shape[1], (at + size, tensor.shape)
                ap = tensor[0:parts, at:at + size]
                names = "abcd"[:len(shape)]
                if len(shape) == 1:
                    return ap
                return ap.rearrange(f"p ({' '.join(names)}) -> p {' '.join(names)}",
                                    **{k: s for k, s in zip(names[1:], shape[1:])})
            return piece

        block = ctx.enter_context(nc.Block())

        w_prep = sem("w_prep")
        w_main = sem("w_main")
        w_zero = sem("w_zero")
        w_eb = sem("w_eb")
        c_set = sem("c_set")
        c_set2 = sem("c_set2")
        p_mm = sem("p_mm")
        p_cp = sem("p_cp")

        a_in = [sem(f"a_in{i}") for i in range(2)]
        (a_bn, a_mv, a_ve, a_rstd, a_xn, a_res0, a_res, a_T, a_xT, a_Q, a_Qe, a_K, a_Ke, a_V, a_Ve,
         a_S, a_mx, a_sub, a_exp, a_sum, a_rcp, a_An, a_AT, a_ATe, a_AV, a_y) = [
            sem(s) for s in ("a_bn a_mv a_ve a_rstd a_xn a_res0 a_res a_T a_xT a_Q a_Qe a_K a_Ke a_V a_Ve "
                             "a_S a_mx a_sub a_exp a_sum a_rcp a_An a_AT a_ATe a_AV a_y").split()]
        (b_bn, b_mv, b_ve, b_rstd, b_yn, b_T, b_ynT, b_H, b_h, b_bn2, b_mv2, b_ve2, b_rstd2, b_x, b_res,
         b_T2, b_xT, b_Q, b_q, b_F, b_pw, b_P) = [
            sem(s) for s in ("b_bn b_mv b_ve b_rstd b_yn b_T b_ynT b_H b_h b_bn2 b_mv2 b_ve2 b_rstd2 b_x b_res "
                             "b_T2 b_xT b_Q b_q b_F b_pw b_P").split()]
        b_sc, c_sc, d_sc = sem("b_sc"), sem("c_sc"), sem("d_sc")
        k_mm, k_cp, k_own = sem("k_mm"), sem("k_cp"), sem("k_own")
        (c_G, c_I, c_h, c_bn, c_mv, c_ve, c_rstd, c_x, c_T, c_xT, c_L, c_lg, c_m8, c_sel, c_mr, c_sub, c_exp,
         c_sum, c_cu, c_c, c_CT, c_cT, c_B, c_hb, c_E, c_stt, c_act, c_add1, c_add2, c_out) = [
            sem(s) for s in ("c_G c_I c_h c_bn c_mv c_ve c_rstd c_x c_T c_xT c_L c_lg c_m8 c_sel c_mr c_sub "
                             "c_exp c_sum c_cu c_c c_CT c_cT c_B c_hb c_E c_stt c_act c_add1 c_add2 "
                             "c_out").split()]
        (d_bn, d_mv, d_ve, d_rstd, d_x, d_T, d_xT, d_G, d_E, d_O, d_rcp, d_h, d_bn2, d_mv2, d_ve2, d_rstd2,
         d_x2, d_T2, d_xT2, d_L, d_mx, d_sub, d_exp, d_sum, d_rcp2, d_S) = [
            sem(s) for s in ("d_bn d_mv d_ve d_rstd d_x d_T d_xT d_G d_E d_O d_rcp d_h d_bn2 d_mv2 d_ve2 "
                             "d_rstd2 d_x2 d_T2 d_xT2 d_L d_mx d_sub d_exp d_sum d_rcp2 d_S").split()]
        (t_mm, t_cp, t_id, t_mm2, t_slot, t_set) = [
            sem(s) for s in "t_mm t_cp t_id t_mm2 t_slot t_set".split()]
        t_own = [sem(f"t_own{i}") for i in range(2)]
        (e_bn, e_mv, e_ve, e_rstd, e_x, e_xh, e_xl, e_P, e_PG, e_X, e_xe, e_PT, e_PTe, e_H, e_hm, e_V, e_v, e_VT, e_vt,
         e_O, e_o) = [
            sem(s) for s in ("e_bn e_mv e_ve e_rstd e_x e_xh e_xl e_P e_PG e_X e_xe e_PT e_PTe e_H e_hm e_V e_v e_VT "
                             "e_vt e_O e_o").split()]
        e_out = [sem(f"e_out{i}") for i in range(2)]

        piece = carve(wide, 11376)
        wv = piece(D, H, D)
        wo = piece(D, H, D)
        wvT = piece(D, H, D)
        bvcol = piece(D, H)
        bvwide = piece(D, H, P)
        insT = piece(NI, D)
        ninv = piece(NI, 1)
        insmean = piece(D, 1)
        inswide = piece(D, D)
        inssel = piece(D, C * E * C * E)
        rmod = piece(D, E)
        gam_w = piece(E, D)
        gamT = piece(D, C, E)
        gamrow = piece(D, E)
        gamcol = piece(C * E, 1)
        beta = piece(D, E, D)
        ebz = piece(C * E, C, D)
        borow = piece(P, D)
        b1row = piece(P, D)

        piece = carve(wide)
        A_xn = [piece(128, 3, D) for _ in range(2)]
        A_xT = [piece(D, KV + TP) for _ in range(2)]
        A_QT = [piece(D, H, TP) for _ in range(2)]
        A_KT = [piece(D, H, KV) for _ in range(2)]
        A_xk = [piece(KV, D) for _ in range(2)]
        A_xq = [piece(P, C, D) for _ in range(2)]
        A_V = [piece(KV, H, D) for _ in range(4)]
        A_A = [[piece(P, H, KV) for _ in range(C)] for _ in range(2)]
        A_AT = [piece(KV, C, H, P) for _ in range(2)]
        assert taken[0] <= 11376
        piece = carve(narrow)
        A_st = [piece(128, 3, 6) for _ in range(2)]
        A_mv = [piece(128, 3, 2) for _ in range(2)]
        A_ve = [piece(128, 3) for _ in range(2)]
        A_rstd = [piece(128, 3) for _ in range(2)]
        A_mx = [piece(P, C, H) for _ in range(2)]
        A_sm = [piece(P, C, H) for _ in range(2)]
        A_rc = [piece(P, C, H) for _ in range(2)]

        B_st = [piece(P, C, 6) for _ in range(2)]
        B_mv = [piece(P, C, 2) for _ in range(2)]
        B_ve = [piece(P, 2, C) for _ in range(2)]
        B_sc = [piece(P, 2, C) for _ in range(2)]
        B_st2 = [piece(P, C, 6) for _ in range(2)]
        B_mv2 = [piece(P, C, 2) for _ in range(2)]
        B_ve2 = [piece(P, C) for _ in range(2)]
        B_rstd2 = [piece(P, C) for _ in range(2)]
        B_pw = [piece(NF, 1) for _ in range(2)]
        B_yn = [piece(P, C, D) for _ in range(2)]
        B_ynT = [piece(D, TP) for _ in range(2)]
        B_h = [piece(P, C, D) for _ in range(2)]
        B_x = [piece(P, C, D) for _ in range(2)]
        B_xT = [piece(D, TP) for _ in range(2)]
        B_q = [piece(P, C, D) for _ in range(2)]
        B_junk = piece(NF, 2 * D)
        spectra = wide[0:NF, 0:N * 2 * D].rearrange("p (n r d) -> p n r d", n=N, r=2)

        piece = carve(narrow)
        K_cr = piece(N, NF - 1 + 8 - PAIRS)
        K_m8 = piece(N, 8)
        K_sel = piece(N, 8)
        K_mr = piece(N, NF - 1 + 8 - PAIRS)
        K_w = piece(N, NF)
        K_wT = piece(NF, N)

        piece = carve(narrow)
        C_st = [piece(P, C, 6) for _ in range(2)]
        C_mv = [piece(P, C, 2) for _ in range(2)]
        C_ve = [piece(P, 2, C) for _ in range(2)]
        C_sc = [piece(P, 2, C) for _ in range(2)]
        C_lg = [piece(P, C, E + 6) for _ in range(2)]
        C_m8 = [piece(P, C, 8) for _ in range(2)]
        C_sel = [piece(P, C, 8) for _ in range(2)]
        C_mr = [piece(P, C, E + 6) for _ in range(2)]
        C_ex = [piece(P, C, E) for _ in range(2)]
        C_sm = [piece(P, C) for _ in range(2)]
        C_rc = [piece(P, C) for _ in range(2)]
        C_c = [piece(P, C, E) for _ in range(2)]
        C_cT = [piece(C * E, P) for _ in range(2)]
        C_G = [piece(NF, 2, D) for _ in range(2)]
        C_h = [piece(P, C, D) for _ in range(4)]
        C_x = [piece(P, C, D) for _ in range(2)]
        C_xT = [piece(D, TP) for _ in range(4)]
        C_t = piece(P, C, E // 2, D)
        C_u = piece(P, C, 2, D)

        piece = carve(narrow)
        D_st = [piece(P, C, 6) for _ in range(2)]
        D_mv = [piece(P, C, 2) for _ in range(2)]
        D_ve = [piece(P, 2, C) for _ in range(2)]
        D_sc = [piece(P, 2, C) for _ in range(2)]
        D_st2 = [piece(P, C, 6) for _ in range(2)]
        D_mv2 = [piece(P, C, 2) for _ in range(2)]
        D_ve2 = [piece(P, C) for _ in range(2)]
        D_rstd2 = [piece(P, C) for _ in range(2)]
        D_rc = [piece(P, C) for _ in range(2)]
        D_mx = [piece(P, C) for _ in range(2)]
        D_sm = [piece(P, C) for _ in range(2)]
        D_rc2 = [piece(P, C) for _ in range(2)]
        D_lg = [piece(P, C, E) for _ in range(2)]
        D_x = [piece(P, C, D + 1) for _ in range(4)]
        D_xT = [piece(D, TP) for _ in range(2)]
        D_E = [piece(P, C, TP) for _ in range(2)]
        D_x2 = [piece(P, C, D) for _ in range(2)]
        D_xT2 = [piece(D, TP) for _ in range(2)]

        GB = 128 // E
        NG = (N + GB - 1) // GB
        piece = carve(narrow)
        T_s = [piece(128, T + 3) for _ in range(2)]
        T_w = [piece(128, T + 3) for _ in range(2)]
        T_m8 = [piece(128, 8) for _ in range(2)]
        T_pos = [piece(128, T) for _ in range(2)]
        T_id = [piece(128, TP) for _ in range(2)]
        T_one = piece(128, T)

        piece = carve(wide)
        E_PT = [piece(KB, C, NB, P) for _ in range(8)]
        E_xe = [piece(D, E, Q4, K) for _ in range(2)]
        E_vt = [piece(D, Q4, E, K) for _ in range(2)]
        piece = carve(narrow)
        E_st = [piece(P, C, 6) for _ in range(2)]
        E_mv = [piece(P, C, 2) for _ in range(2)]
        E_ve = [piece(P, C) for _ in range(2)]
        E_rstd = [piece(P, C) for _ in range(2)]
        E_x = [piece(P, C, D) for _ in range(2)]
        E_PG = [piece(P, C, E, K) for _ in range(1)]
        E_hm = [piece(D, FC, Q4 * K) for _ in range(2)]
        E_v = piece(KB, NB, D)
        def rows(ap, parts):
            return ap.partition_broadcast(parts)

        @block.sync
        def _(sp):
            prep = [(wv, Wv.rearrange("h d e -> d h e")), (wo, Wo.rearrange("(h e) d -> e h d", h=H)),
                    (bvcol, bv.rearrange("h e -> e h")), (insT, ins[0]),
                    (rmod, rmod_w), (gam_w, gamma_w), (beta, beta_w.rearrange("e h d -> h e d")),
                    (borow, rows(bo, P)), (b1row, rows(b1, P)),
                    (wx[:, :, :], expert_w.rearrange("e l d -> l e d"))]
            for dst, src in prep:
                sp.dma_start(dst, src, allow_slow_non_contiguous=True).then_inc(w_prep, 16)
            main = [(wq[:, :, :], Wq.rearrange("h d e -> d h e")), (wk[:, :, :], Wk.rearrange("h d e -> d h e")),
                    (cols[:, 0:1], g1.unsqueeze(1)), (cols[:, 1:2], b1.unsqueeze(1)),
                    (cols[:, 2:3], g2.unsqueeze(1)), (cols[:, 3:4], b2.unsqueeze(1)),
                    (cols[:, 4:4 + H], bq.rearrange("h e -> e h")), (cols[:, 4 + H:4 + 2 * H], bk.rearrange("h e -> e h")),
                    (g1row[:, :], rows(g1, P)), (bfrow[:, :], rows(bf, P)), (barow[:, :], rows(ba, P)),
                    (wf[:, :], Wf), (wa[:, :], Wa), (gatew[:, :], gate_w), (wg[:, :], Wg),
                    (fwd[:, 0, :, :], tab_fwd_cos.rearrange("(c p) f -> p c f", c=C)),
                    (fwd[:, 1, :, :], tab_fwd_sin.rearrange("(c p) f -> p c f", c=C)),
                    (inv[:, 0, :], tab_inv_cos), (inv[:, 1, :], tab_inv_sin),
                    (w1[:, :, :], W1.rearrange("e d f -> d e f")),
                    (w2[:, :, :, :], W2.rearrange("e (c f) d -> f e c d", c=FC)),
                    (b1col[:, :, :], eb1.rearrange("e (c f) -> f e c", c=FC)),
                    (b2col[:, :], eb2.rearrange("e d -> d e"))]
            for dst, src in main:
                sp.dma_start(dst, src, allow_slow_non_contiguous=True).then_inc(w_main, 16)
            sp.wait_ge(w_zero, 1)
            for c in range(C):
                sp.dma_start(ebz[c * E:(c + 1) * E, c, :], expert_b).then_inc(w_eb, 16)

            def load(t, r):
                if not is_live(t, N):
                    return
                s = r % 2
                wait(sp, a_xn, t - 1)
                if isinstance(t, int) and t < 2:
                    sp.wait_ge(c_set, 1)
                sp.dma_start(A_xk[s], x[t, 0:KV, :]).then_inc(a_in[s], 16)
                for c in range(C):
                    m = P if c < C - 1 else LAST
                    sp.dma_start(A_xq[s][0:m, c, :], x[t, KV + c * P:KV + c * P + m, :]).then_inc(a_in[s], 16)
            walk(sp, N, LEAD, U, 0, load)

            def store(t, r):
                b = t - 9
                if not is_live(b, N):
                    return
                s = (r - 9) % 2
                wait(sp, e_o, b + 1)
                for c in range(C):
                    m = P if c < C - 1 else LAST
                    sp.dma_start(out[b, c * P:c * P + m, :], h[0:m, b, c, :]).then_inc(e_out[s], 16)
            walk(sp, N, LEADE, UE, TAILE, store)
            for s in range(2):
                sp.wait_ge(e_out[s], 16 * C * (N // 2))

        @block.gpsimd
        def _(pool):
            for s in range(2):
                nc.gpsimd.memset(A_xq[s], 0.0)
            nc.gpsimd.memset(epsilon[:, :], EPS)
            nc.gpsimd.memset(nought[:, :], 0.0)
            nc.gpsimd.memset(mhalf[:, :], -0.5).then_inc(c_set, 1)
            nc.gpsimd.memset(ebz, 0.0).then_inc(w_zero, 1)
            nc.gpsimd.memset(mshift[:, :], -SHIFT)
            nc.gpsimd.memset(inssel, 0.0)
            nc.gpsimd.memset(ninv, 1.0 / NI)
            for s in range(2):
                nc.gpsimd.memset(A_mv[s], 1.0)
            nc.gpsimd.iota(slotno[:, :], [[1, K]], base=0, channel_multiplier=0,
                           allow_small_or_imprecise_dtypes=True)
            nc.gpsimd.memset(ident[:, :], 0.0).then_inc(c_set, 1)
            pool.wait_ge(c_set, 2)
            nc.gpsimd.affine_select(out=ident[:, :], in_=ident[:, :], compare_op=ALU.not_equal, fill=1.0, base=0,
                                    pattern=[[-1, 128]], channel_multiplier=1).then_inc(c_set, 1)
            pool.wait_ge(w_prep, 16 * 10)
            nc.gpsimd.tensor_tensor(b1row, b1row, borow, ALU.add).then_inc(c_set, 1)

            def root(b, var, ve, rstd, e_sem, r_sem, n_mv, freed):
                pool.wait_ge(n_mv, b + 1)
                wait(pool, freed, b - 1)
                nc.gpsimd.tensor_tensor(ve, var, epsilon[0:ve.shape[0], 0:ve.shape[1]], ALU.add).then_inc(e_sem, 1)
                pool.wait_ge(e_sem, b + 1)
                nc.gpsimd.tensor_tensor(rstd, ve, mhalf[0:ve.shape[0], 0:ve.shape[1]], ALU.pow).then_inc(r_sem, 1)

            def root_and_bias(b, mv, ve, scale, e_sem, r_sem, s_sem, n_mv, freed):
                pool.wait_ge(n_mv, b + 1)
                wait(pool, freed, b - 1)
                nc.gpsimd.tensor_tensor(ve[:, 1, :], nought[0:P, 0:C], mv[:, :, 0], ALU.subtract)
                nc.gpsimd.tensor_tensor(ve[:, 0, :], mv[:, :, 1], epsilon[0:P, 0:C], ALU.add).then_inc(e_sem, 1)
                pool.wait_ge(e_sem, b + 1)
                nc.gpsimd.tensor_tensor(scale[:, 0, :], ve[:, 0, :], mhalf[0:P, 0:C], ALU.pow).then_inc(r_sem, 1)
                pool.wait_ge(r_sem, b + 1)
                nc.gpsimd.tensor_tensor(scale[:, 1, :], ve[:, 1, :], scale[:, 0, :], ALU.mult).then_inc(s_sem, 1)

            def phase_a(t, r):
                if is_live(t, N):
                    s = r % 2
                    root(t, A_mv[s][:, :, 1], A_ve[s], A_rstd[s], a_ve, a_rstd, a_mv, a_xn)
                    wait_apart(pool, a_xn, t + 1, c_set)
                    if isinstance(t, int) and t == 0:
                        pool.wait_ge(w_main, 16 * 23)
                        pool.wait_ge(p_cp, 5)
                    nc.gpsimd.tensor_tensor(h[:, t], A_xn[s][0:P, 1:3, :],
                                            g1row[:, :].unsqueeze(1).broadcast_to([P, C, D]),
                                            ALU.mult).then_inc(a_res0, 1)
                    wait_apart(pool, a_res0, t + 1, c_set)
                    nc.gpsimd.tensor_tensor(h[:, t], h[:, t], crow[:, :].unsqueeze(1).broadcast_to([P, C, D]),
                                            ALU.add).then_inc(a_res, 1)
                b = t - 3
                if is_live(b, N):
                    s = (r - 3) % 2
                    pool.wait_ge(a_rcp, b + 1)
                    for c in range(C):
                        nc.gpsimd.tensor_tensor(A_A[s][c], A_A[s][c],
                                                A_rc[s][:, c, :].unsqueeze(2).broadcast_to([P, H, KV]),
                                                ALU.mult).then_inc(a_An, 1)
            walk(pool, N, LEAD, U, TAIL, phase_a)

            def phase_b(t, r):
                if is_live(t, N):
                    s = r % 2
                    root_and_bias(t, B_mv[s], B_ve[s], B_sc[s], b_ve, b_rstd, b_sc, b_mv, b_yn)
                b = t - 2
                if is_live(b, N):
                    s = (r - 2) % 2
                    root(b, B_mv2[s][:, :, 1], B_ve2[s], B_rstd2[s], b_ve2, b_rstd2, b_mv2, b_x)
                b = t - 5
                if is_live(b, N):
                    s = (r - 5) % 2
                    wait_apart(pool, b_pw, b + 1, c_set)
                    nc.gpsimd.tensor_copy(power[:, b:b + 1] if isinstance(b, int) else power[:, bass.ds(b, 1)],
                                          B_pw[s]).then_inc(b_P, 1)
            walk(pool, N, LEAD, U, TAIL, phase_b)

            def phase_c(t, r):
                b = t - 1
                if is_live(b, N):
                    s = (r - 1) % 2
                    root_and_bias(b, C_mv[s], C_ve[s], C_sc[s], c_ve, c_rstd, c_sc, c_mv, c_x)
                b = t - 4
                if is_live(b, N):
                    pool.wait_ge(c_act, C * (b + 1))
                    wait(pool, c_out, b)
                    half = E // 4
                    nc.gpsimd.tensor_tensor(C_u, C_t[:, :, 0:half, :], C_t[:, :, half:, :], ALU.add)\
                        .then_inc(c_add1, 1)
                    pool.wait_ge(c_add1, b + 1)
                    nc.gpsimd.tensor_tensor(C_u[:, :, 0, :], C_u[:, :, 0, :], C_u[:, :, 1, :], ALU.add)\
                        .then_inc(c_add2, 1)
            walk(pool, N, LEAD, U, TAIL, phase_c)

            def phase_d(t, r):
                if is_live(t, N):
                    s = r % 2
                    root_and_bias(t, D_mv[s], D_ve[s], D_sc[s], d_ve, d_rstd, d_sc, d_mv, d_x)
                b = t - 3
                if is_live(b, N):
                    s = (r - 3) % 2
                    root(b, D_mv2[s][:, :, 1], D_ve2[s], D_rstd2[s], d_ve2, d_rstd2, d_mv2, d_x2)
            walk(pool, N, LEAD, U, TAIL, phase_d)

            def phase_e(t, r):
                if is_live(t, N):
                    s = r % 2
                    root(t, E_mv[s][:, :, 1], E_ve[s], E_rstd[s], e_ve, e_rstd, e_mv, e_x)
                    wait_apart(pool, e_P, C * (t + 1), c_set)
                    wait(pool, e_PT, C * t)
                    for c in range(C):
                        gate = gates[:, c, E * t:E * t + E] if isinstance(t, int) else gates[:, c, bass.ds(t * E, E)]
                        nc.gpsimd.tensor_tensor(E_PG[0][:, c], E_P[s][:, c, :, :],
                                                gate.unsqueeze(2).broadcast_to([P, E, K]),
                                                ALU.mult).then_inc(e_PG, 1)
            walk(pool, N, LEADE, UE, 0, phase_e)

        @block.tensor
        def _(pe):
            mm, tr = nc.tensor.matmul, nc.tensor.transpose

            pe.wait_ge(c_set, 4)
            pe.wait_ge(w_prep, 16 * 10)
            for i in range(H):
                last = tr(bank[0][:, i * D:(i + 1) * D], wv[:, i, :], ident[:, :])
            last.then_inc(p_mm, 1)
            mm(bank[1][:, 0:1], insT, ninv, start=True, stop=True)
            tr(bank[2][:, 0:E], gam_w, ident[0:E, 0:E]).then_inc(p_mm, 1)
            pe.wait_ge(p_cp, 4)
            for i in range(H):
                mm(bank[3][0:P, 0:D], bvwide[:, i, :], wo[:, i, :], start=(i == 0), stop=(i == H - 1))
            for i in range(H):
                last = mm(bank[4][:, i * D:(i + 1) * D], wvT[:, i, :], wo[:, i, :], start=True, stop=True)
            last.then_inc(p_mm, 1)
            mm(bank[5][0:P, 0:E], inswide[:, 0:P], rmod, start=True, stop=True)
            mm(bank[5][0:C * E, 16:17], gamT.rearrange("p c e -> p (c e)"), insmean, start=True, stop=True)
            mm(bank[6][:, 0:E], inswide, gamT[:, 0, :], start=True, stop=True)
            for c in range(C):
                for e in range(E):
                    at = (c * E + e) * C * E
                    last = mm(bank[7][0:C * E, c * D:(c + 1) * D], inssel[:, at:at + C * E], beta[:, e, :],
                              start=(e == 0), stop=(e == E - 1))
            last.then_inc(p_mm, 1)

            def phase_a(t, r):
                if isinstance(t, int) and t == 0:
                    pe.wait_ge(w_main, 16 * 23)
                    pe.wait_ge(p_cp, 10)
                b = t - 2
                if is_live(b, N):
                    s = (r - 2) % 2
                    pe.wait_ge(a_xT, b + 1)
                    for i in range(H):
                        if i == 0:
                            wait(pe, a_Qe, 2 * b - 1)
                            wait(pe, a_ATe, 2 * (b - 2))
                        if i == H // 2:
                            wait(pe, a_Qe, 2 * b)
                            wait(pe, a_y, b - 3)
                        last = mm(bank[1 + i // 2][:, (i % 2) * TP:(i % 2 + 1) * TP], wq[:, i, :],
                                  A_xT[s][:, KV:], start=True, stop=True)
                        if i % 2 == 1:
                            last.then_inc(a_Q, 1)
                b = t - 3
                if is_live(b, N):
                    s = (r - 3) % 2
                    pe.wait_ge(a_Qe, 2 * b + 2)
                    pe.wait_ge(a_Ke, b + 1)
                    for c in range(C):
                        wait(pe, a_sub, 2 * b + c - 1)
                        for i in range(H):
                            last = mm(bank[5 + c][0:P, i * KV:(i + 1) * KV], A_QT[s][:, i, c * P:(c + 1) * P],
                                      A_KT[s][:, i, :], start=True, stop=True)
                        last.then_inc(a_S, 1)
                b = t - 1
                if is_live(b, N):
                    s = (r - 1) % 2
                    pe.wait_ge(a_xn, b + 1)
                    wait(pe, a_xT, b)
                    tr(bank[0][:, 0:KV], A_xn[s][:, 0, :], ident[:, :])
                    for c in range(C):
                        last = tr(bank[0][:, KV + c * P:KV + (c + 1) * P], A_xn[s][0:P, 1 + c, :], ident[0:P, 0:P])
                    last.then_inc(a_T, 1)
                b = t - 4
                if is_live(b, N):
                    s = (r - 4) % 2
                    for c in range(C):
                        pe.wait_ge(a_An, 2 * b + c + 1)
                        wait(pe, a_ATe, 2 * b - 1 + c)
                        if c == 1:
                            pe.wait_ge(a_Qe, min(2 * b + 5, 2 * N) if isinstance(b, int) else 2 * b + 5)
                        for i in range(H):
                            last = tr(bank[7 if c == 0 else 1][:, i * P:(i + 1) * P], A_A[s][c][:, i, :],
                                      ident[0:P, 0:P])
                        last.then_inc(a_AT, 1)
                b = t - 5
                if is_live(b, N):
                    s = (r - 5) % 2
                    pe.wait_ge(a_ATe, 2 * b + 2)
                    pe.wait_ge(a_Ve, b + 1)
                    pe.wait_ge(a_Qe, min(2 * b + 8, 2 * N) if isinstance(b, int) else 2 * b + 8)
                    wait(pe, a_y, b)
                    for c in range(C):
                        for i in range(H):
                            last = mm(bank[2][0:P, c * D:(c + 1) * D], A_AT[s][:, c, i, :],
                                      A_V[(r - 5) % 4][:, i, :], start=(i == 0), stop=(i == H - 1))
                    last.then_inc(a_AV, 1)
                b = t - 2
                if is_live(b, N):
                    s = (r - 2) % 2
                    wait(pe, a_Ke, b)
                    for i in range(H):
                        last = mm(bank[3][:, i * KV:(i + 1) * KV], wk[:, i, :], A_xT[s][:, 0:KV],
                                  start=True, stop=True)
                    last.then_inc(a_K, 1)
                    wait(pe, a_Ve, b)
                    mm(bank[4][:, :], A_xT[s][:, 0:KV], wvo[:, :, :].rearrange("p h d -> p (h d)"),
                       start=True, stop=True).then_inc(a_V, 1)
            walk(pe, N, LEAD, U, TAIL, phase_a)

            def phase_b(t, r):
                if isinstance(t, int) and t == 0:
                    pe.wait_ge(a_y, N)
                b = t - 2
                if is_live(b, N):
                    s = (r - 2) % 2
                    pe.wait_ge(b_ynT, b + 1)
                    wait(pe, b_h, b)
                    for c in range(C):
                        last = mm(bank[1][0:P, c * D:(c + 1) * D], B_ynT[s][:, c * P:(c + 1) * P], wf[:, :],
                                  start=True, stop=True)
                    last.then_inc(b_H, 1)
                b = t - 4
                if is_live(b, N):
                    s = (r - 4) % 2
                    pe.wait_ge(b_xT, b + 1)
                    wait(pe, b_q, b)
                    for c in range(C):
                        last = mm(bank[3][0:P, c * D:(c + 1) * D], B_xT[s][:, c * P:(c + 1) * P], wa[:, :],
                                  start=True, stop=True)
                    last.then_inc(b_Q, 1)
                b = t - 5
                if is_live(b, N):
                    s = (r - 5) % 2
                    pe.wait_ge(b_q, b + 1)
                    wait(pe, b_pw, b)
                    for k in range(2):
                        for c in range(C):
                            last = mm(bank[4][0:NF, k * D:(k + 1) * D], fwd[:, k, c, :], B_q[s][:, c, :],
                                      start=(c == 0), stop=(c == C - 1))
                    last.then_inc(b_F, 1)
                b = t - 1
                if is_live(b, N):
                    s = (r - 1) % 2
                    pe.wait_ge(b_yn, b + 1)
                    wait(pe, b_ynT, b)
                    for c in range(C):
                        last = tr(bank[0][:, c * P:(c + 1) * P], B_yn[s][:, c, :], ident[0:P, 0:P])
                    last.then_inc(b_T, 1)
                b = t - 3
                if is_live(b, N):
                    s = (r - 3) % 2
                    pe.wait_ge(b_x, b + 1)
                    wait(pe, b_xT, b)
                    for c in range(C):
                        last = tr(bank[2][:, c * P:(c + 1) * P], B_x[s][:, c, :], ident[0:P, 0:P])
                    last.then_inc(b_T2, 1)
            walk(pe, N, LEAD, U, TAIL, phase_b)

            pe.wait_ge(b_P, N)
            mm(bank[5][0:N, 0:NF], power[:, :], inv[:, 0, 0:NF], start=True, stop=True).then_inc(k_mm, 1)
            pe.wait_ge(k_cp, 5)
            tr(bank[6][0:NF, 0:N], K_w, ident[0:N, 0:N]).then_inc(k_mm, 1)
            pe.wait_ge(k_cp, 6)
            mm(bank[7][0:NF, 0:N], fwd[:, 0, 0, :], K_wT, start=True, stop=True).then_inc(k_mm, 1)

            def phase_c(t, r):
                if isinstance(t, int) and t == 0:
                    pe.wait_ge(k_cp, 7)
                b = t - 5
                if is_live(b, N):
                    s = (r - 5) % 2
                    pe.wait_ge(c_cT, b + 1)
                    for c in range(C):
                        last = mm(bank[7][0:P, 128 + c * D:128 + (c + 1) * D], C_cT[s], bmod[:, c, :],
                                  start=True, stop=True)
                    last.then_inc(c_B, 1)
                b = t - 1
                if is_live(b, N):
                    s = (r - 1) % 2
                    pe.wait_ge(c_G, b + 1)
                    wait(pe, c_h, b)
                    for c in range(C):
                        for k in range(2):
                            last = mm(bank[0][0:P, c * D:(c + 1) * D], inv[:, k, c * P:(c + 1) * P],
                                      C_G[s][:, k, :], start=(k == 0), stop=(k == 1))
                    last.then_inc(c_I, 1)
                b = t - 3
                if is_live(b, N):
                    s = (r - 3) % 4
                    pe.wait_ge(c_xT, b + 1)
                    wait(pe, c_lg, b)
                    for c in range(C):
                        last = mm(bank[2][0:P, c * E:(c + 1) * E], C_xT[s][:, c * P:(c + 1) * P], gatew[:, :],
                                  start=True, stop=True)
                    last.then_inc(c_L, 1)
                b = t - 4
                if is_live(b, N):
                    for c in range(C):
                        wait(pe, c_stt, E * b - 1 + c)
                        mm(bank[3 + 2 * c][0:P, :], C_xT[(r - 4) % 4][:, c * P:(c + 1) * P],
                           wx[:, 0:E // 2, :].rearrange("p e d -> p (e d)"),
                           start=True, stop=True).then_inc(c_E, 1)
                b = t - 4
                if is_live(b, N):
                    s = (r - 4) % 2
                    pe.wait_ge(c_c, b + 1)
                    wait(pe, c_hb, b)
                    tr(bank[7][0:C * E, 0:P], C_c[s].rearrange("p c e -> p (c e)"), ident[0:P, 0:P])\
                        .then_inc(c_CT, 1)
                    for c in range(C):
                        wait(pe, c_act, C * (b - 1) + c + 1)
                        mm(bank[4 + 2 * c][0:P, :], C_xT[(r - 4) % 4][:, c * P:(c + 1) * P],
                           wx[:, E // 2:E, :].rearrange("p e d -> p (e d)"),
                           start=True, stop=True).then_inc(c_E, 1)
                b = t - 2
                if is_live(b, N):
                    s = (r - 2) % 2
                    pe.wait_ge(c_x, b + 1)
                    wait(pe, c_xT, b)
                    for c in range(C):
                        last = tr(bank[1][:, c * P:(c + 1) * P], C_x[s][:, c, :], ident[0:P, 0:P])
                    last.then_inc(c_T, 1)
            walk(pe, N, LEAD, U, TAIL, phase_c)

            def phase_d(t, r):
                if isinstance(t, int) and t == 0:
                    pe.wait_ge(c_out, N)
                b = t - 5
                if is_live(b, N):
                    s = (r - 5) % 2
                    pe.wait_ge(d_x2, b + 1)
                    wait(pe, d_xT2, b)
                    for c in range(C):
                        last = tr(bank[3][:, c * P:(c + 1) * P], D_x2[s][:, c, :], ident[0:P, 0:P])
                    last.then_inc(d_T2, 1)
                b = t - 3
                if is_live(b, N):
                    s = (r - 3) % 2
                    pe.wait_ge(d_E, b + 1)
                    wait(pe, d_h, b)
                    for c in range(C):
                        for k in range(C):
                            m = P if k < C - 1 else LAST
                            last = mm(bank[2][0:P, c * (D + 1):(c + 1) * (D + 1)],
                                      D_E[s][0:m, k, c * P:(c + 1) * P], D_x[(r - 3) % 4][0:m, k, :],
                                      start=(k == 0), stop=(k == C - 1))
                    last.then_inc(d_O, 1)
                b = t - 2
                if is_live(b, N):
                    s = (r - 2) % 2
                    pe.wait_ge(d_xT, b + 1)
                    wait(pe, d_E, b)
                    for c in range(C):
                        last = mm(bank[1][0:P, c * TP:(c + 1) * TP], D_xT[s][:, c * P:(c + 1) * P], D_xT[s],
                                  start=True, stop=True)
                    last.then_inc(d_G, 1)
                b = t - 1
                if is_live(b, N):
                    s = (r - 1) % 2
                    pe.wait_ge(d_x, b + 1)
                    wait(pe, d_xT, b)
                    for c in range(C):
                        last = tr(bank[0][:, c * P:(c + 1) * P], D_x[(r - 1) % 4][:, c, 0:D], ident[0:P, 0:P])
                    last.then_inc(d_T, 1)
                b = t - 5
                if is_live(b, N):
                    s = (r - 5) % 2
                    pe.wait_ge(d_xT2, b + 1)
                    wait(pe, d_sub, b)
                    for c in range(C):
                        last = mm(bank[4][0:P, c * E:(c + 1) * E], D_xT2[s][:, c * P:(c + 1) * P], wg[:, :],
                                  start=True, stop=True)
                    last.then_inc(d_L, 1)
            walk(pe, N, LEAD, U, TAIL, phase_d)

            pe.wait_ge(d_S, N)
            for g in range(NG):
                rows_g = min(GB, N - g * GB) * E
                if g >= 2:
                    pe.wait_ge(t_cp, g - 1)
                for c in range(C):
                    last = tr(bank[g % 2][0:rows_g, c * P:(c + 1) * P], gates[:, c, g * 128:g * 128 + rows_g],
                              ident[0:P, 0:P])
                last.then_inc(t_mm, 1)
            for g in range(NG):
                rows_g = min(GB, N - g * GB) * E
                pe.wait_ge(t_id, g + 1)
                if g >= 2:
                    pe.wait_ge(t_slot, g - 1)
                for c in range(C):
                    last = tr(bank[2 + g % 2][0:P, c * 128:c * 128 + rows_g], T_id[g % 2][0:rows_g, c * P:(c + 1) * P],
                              ident[0:rows_g, 0:rows_g])
                last.then_inc(t_mm2, 1)

            def phase_e(t, r):
                if isinstance(t, int) and t == 0:
                    pe.wait_ge(t_slot, NG)
                b = t - 9
                if is_live(b, N):
                    q = ((r - 9) % 8) // 4
                    if r % 4 == 1:
                        pe.wait_ge(e_v, (b + 4) * 2)
                    wait(pe, e_vt, b)
                    for k in range(NB):
                        last = tr(bank[6][0:KB, k * D:(k + 1) * D],
                                  E_vt[q][:, (r - 9) % 4, 2 * k:2 * k + 2, :].rearrange("p e k -> p (e k)"),
                                  ident[:, :])
                    last.then_inc(e_VT, 1)
                q5 = t - 5 - (r - 5) % 4
                live_q = is_live(t - 5, N)
                qs = ((r - 5) % 8) // 4
                e0 = 2 * ((r - 5) % 4)
                u = t - 5

                def up(k):
                    pe.wait_ge(e_xe, q5 + 4)
                    wait(pe, e_hm, 2 * (u * 2 + k) - 2)
                    for f in range(FC):
                        last = mm(bank[3 + k][:, f * Q4 * K:(f + 1) * Q4 * K], w1[:, e0 + k, f * D:(f + 1) * D],
                                  E_xe[qs][:, e0 + k].rearrange("p b k -> p (b k)"), start=True, stop=True)
                    last.then_inc(e_H, 1)

                def down(k):
                    pe.wait_ge(e_hm, 2 * (u * 2 + k) + 2)
                    wait(pe, e_v, u * 2 + k)
                    for f in range(FC):
                        last = mm(bank[5][:, 0:Q4 * K], w2[:, e0 + k, f, :], E_hm[k][:, f, :],
                                  start=(f == 0), stop=(f == FC - 1))
                    last.then_inc(e_V, 1)

                if live_q:
                    up(0)
                b = t - 1
                if is_live(b, N):
                    s = (r - 1) % 2
                    pe.wait_ge(e_xl, b + 1)
                    pe.wait_ge(e_P, C * b + 2)
                    wait(pe, e_xe, b)
                    for c in range(C):
                        for half in (E_xh, E_xl):
                            last = mm(bank[0][:, 0:EK], half[s][:, c, :], E_P[s][:, c, :, :].rearrange("p e k -> p (e k)"),
                                      start=(c == 0 and half is E_xh), stop=(c == C - 1 and half is E_xl))
                    last.then_inc(e_X, 1)
                if live_q:
                    up(1)
                b = t - 9
                if is_live(b, N):
                    pe.wait_ge(e_vt, b + 1)
                    wait(pe, e_o, b)
                    for c in range(C):
                        for k in range(NB):
                            last = mm(bank[7][0:P, c * D:(c + 1) * D], E_PT[(r - 9) % 8][:, c, k, :], E_v[:, k, :],
                                      start=(k == 0), stop=(k == NB - 1))
                    last.then_inc(e_O, 1)
                if live_q:
                    down(0)
                b = t - 1
                if is_live(b, N):
                    for c in range(C):
                        pe.wait_ge(e_PG, C * b + c + 1)
                        wait(pe, e_PTe, C * (b - 1) + c + 1)
                        for k in range(NB):
                            last = tr(bank[1 + c][0:KB, k * P:(k + 1) * P],
                                      E_PG[0][:, c, 2 * k:2 * k + 2, :].rearrange("p e k -> p (e k)"),
                                      ident[0:P, 0:P])
                        last.then_inc(e_PT, 1)
                if live_q:
                    down(1)
            walk(pe, N, LEADE, UE, TAILE, phase_e)

        @block.scalar
        def _(act):
            fn, copy = nc.scalar.activation, nc.scalar.copy

            def normalise(b, src, dst, scale, s_scale, s_x):
                wait_apart(act, s_scale, b + 1, c_set)
                for c in range(C):
                    last = fn(dst[c], src[:, c, :], ACT.Identity, bias=scale[:, 1, c:c + 1], scale=scale[:, 0, c:c + 1])
                last.then_inc(s_x, 1)

            def phase_a(t, r):
                if isinstance(t, int) and t == 0:
                    act.wait_ge(w_main, 16 * 23)
                b = t - 3
                if is_live(b, N):
                    s = (r - 3) % 2
                    for c in range(C):
                        act.wait_ge(a_sub, 2 * b + c + 1)
                        fn(A_A[s][c], A_A[s][c], ACT.Exp, scale=SCALE).then_inc(a_exp, 1)
                b = t - 1
                if is_live(b, N):
                    s = (r - 1) % 2
                    act.wait_ge(a_T, b + 1)
                    wait(act, a_V, b - 1)
                    fn(A_xT[s], bank[0][:, 0:KV + TP], ACT.Identity, bias=cols[:, 1:2], scale=cols[:, 0:1])\
                        .then_inc(a_xT, 1)
                b = t - 4
                if is_live(b, N):
                    s = (r - 4) % 2
                    for c in range(C):
                        act.wait_ge(a_AT, 2 * b + c + 1)
                        wait(act, a_AV, b - 1)
                        copy(A_AT[s][:, c].rearrange("p h k -> p (h k)"), bank[7 if c == 0 else 1][:, 0:H * P])\
                            .then_inc(a_ATe, 1)
                b = t - 2
                if is_live(b, N):
                    act.wait_ge(a_V, b + 1)
                    wait(act, a_AV, b - 3)
                    copy(A_V[(r - 2) % 4].rearrange("p h d -> p (h d)"), bank[4][:, :]).then_inc(a_Ve, 1)
            walk(act, N, LEAD, U, TAIL, phase_a)

            def phase_b(t, r):
                if isinstance(t, int) and t == 0:
                    act.wait_ge(a_y, N)
                b = t - 1
                if is_live(b, N):
                    s = (r - 1) % 2
                    wait(act, b_T, b - 1)
                    normalise(b, h[:, b], [B_yn[s][:, c, :] for c in range(C)], B_sc[s], b_sc, b_yn)
                b = t - 1
                if is_live(b, N):
                    s = (r - 1) % 2
                    act.wait_ge(b_T, b + 1)
                    wait(act, b_H, b - 1)
                    fn(B_ynT[s], bank[0][:, 0:TP], ACT.Identity, bias=cols[:, 3:4], scale=cols[:, 2:3])\
                        .then_inc(b_ynT, 1)
                b = t - 3
                if is_live(b, N):
                    s = (r - 3) % 2
                    act.wait_ge(b_T2, b + 1)
                    wait(act, b_Q, b - 1)
                    copy(B_xT[s], bank[2][:, 0:TP]).then_inc(b_xT, 1)
                b = t - 5
                if is_live(b, N):
                    s = (r - 5) % 2
                    act.wait_ge(b_F, b + 1)
                    copy(spectra[:, b].rearrange("p r d -> p (r d)"), bank[4][0:NF, 0:2 * D])
                    wait(act, b_P, b - 1)
                    wait(act, b_pw, b)
                    fn(B_junk, bank[4][0:NF, 0:2 * D], ACT.Square, accum_out=B_pw[s]).then_inc(b_pw, 1)
            walk(act, N, LEAD, U, TAIL, phase_b)

            def phase_c(t, r):
                if isinstance(t, int) and t == 0:
                    act.wait_ge(k_cp, 7)
                b = t - 2
                if is_live(b, N):
                    s = (r - 2) % 2
                    wait(act, c_T, b - 1)
                    normalise(b, C_h[(r - 2) % 4], [C_x[s][:, c, :] for c in range(C)], C_sc[s], c_sc, c_x)
                if is_live(t, N):
                    s = r % 2
                    wait(act, c_I, t - 1)
                    factor = wfreq[:, t:t + 1] if isinstance(t, int) else wfreq[:, bass.ds(t, 1)]
                    fn(C_G[s], spectra[:, t], ACT.Copy, scale=factor).then_inc(c_G, 1)
                b = t - 4
                if is_live(b, N):
                    s = (r - 4) % 2
                    act.wait_ge(c_CT, b + 1)
                    wait(act, c_B, b - 1)
                    copy(C_cT[s], bank[7][0:C * E, 0:P]).then_inc(c_cT, 1)
                b = t - 4
                if is_live(b, N):
                    s = (r - 4) % 2
                    wait(act, c_add1, b)
                    for c in range(C):
                        act.wait_ge(c_E, 4 * b + c + 3)
                        for e in range(E // 2):
                            last = fn(C_t[:, c, e, :], bank[4 + 2 * c][0:P, e * D:(e + 1) * D], ACT.Copy,
                                      scale=C_c[s][:, c, E // 2 + e:E // 2 + e + 1])
                        last.then_inc(c_act, 1)
                b = t - 2
                if is_live(b, N):
                    act.wait_ge(c_T, b + 1)
                    wait(act, c_E, 4 * (b - 3))
                    copy(C_xT[(r - 2) % 4], bank[1][:, 0:TP]).then_inc(c_xT, 1)
                b = t - 3
                if is_live(b, N):
                    s = (r - 3) % 2
                    act.wait_ge(c_sub, b + 1)
                    fn(C_ex[s], C_ex[s], ACT.Exp).then_inc(c_exp, 1)
            walk(act, N, LEAD, U, TAIL, phase_c)

            def phase_d(t, r):
                if isinstance(t, int) and t == 0:
                    act.wait_ge(c_out, N)
                    act.wait_ge(c_set2, 3)
                b = t - 5
                if is_live(b, N):
                    s = (r - 5) % 2
                    act.wait_ge(d_T2, b + 1)
                    wait(act, d_L, b - 1)
                    copy(D_xT2[s], bank[3][:, 0:TP]).then_inc(d_xT2, 1)
                b = t - 1
                if is_live(b, N):
                    s = (r - 1) % 2
                    wait(act, d_T, b - 3)
                    wait(act, d_O, b - 3)
                    normalise(b, h[:, b], [D_x[(r - 1) % 4][:, c, 0:D] for c in range(C)], D_sc[s], d_sc, d_x)
                b = t - 6
                if is_live(b, N):
                    s = (r - 6) % 2
                    act.wait_ge(d_sub, b + 1)
                    fn(D_lg[s], D_lg[s], ACT.Exp).then_inc(d_exp, 1)
                b = t - 2
                if is_live(b, N):
                    s = (r - 2) % 2
                    act.wait_ge(d_G, b + 1)
                    wait(act, d_O, b - 1)
                    fn(D_E[s].rearrange("p c k -> p (c k)"), bank[1][0:P, 0:C * TP], ACT.Exp,
                       bias=mshift[0:P, :]).then_inc(d_E, 1)
                b = t - 1
                if is_live(b, N):
                    s = (r - 1) % 2
                    act.wait_ge(d_T, b + 1)
                    wait(act, d_G, b - 1)
                    copy(D_xT[s], bank[0][:, 0:TP]).then_inc(d_xT, 1)
            walk(act, N, LEAD, U, TAIL, phase_d)

            def phase_e(t, r):
                if isinstance(t, int) and t == 0:
                    act.wait_ge(t_slot, NG)
                b = t - 1
                if is_live(b, N):
                    act.wait_ge(e_x, b + 1)
                    wait(act, e_X, b - 1)
                    copy(E_xh[(r - 1) % 2][:, :, :], E_x[(r - 1) % 2]).then_inc(e_xh, 1)
                u = t - 5
                e0 = 2 * ((r - 5) % 4)

                def gelu(k):
                    act.wait_ge(e_H, u * 2 + k + 1)
                    wait(act, e_V, u * 2 + k - 1)
                    for f in range(FC):
                        fn(E_hm[k][:, f, :], bank[3 + k][:, f * Q4 * K:(f + 1) * Q4 * K], ACT.Gelu,
                           bias=b1col[:, e0 + k, f:f + 1], scale=1.0).then_inc(e_hm, 1)

                if is_live(u, N):
                    gelu(0)
                b = t - 1
                if is_live(b, N):
                    q = ((r - 1) % 8) // 4
                    act.wait_ge(e_X, b + 1)
                    if (r - 1) % 4 == 0:
                        wait(act, e_H, 2 * (b - 4))
                    copy(E_xe[q][:, :, (r - 1) % 4, :], bank[0][:, 0:EK].rearrange("p (e k) -> p e k", e=E))\
                        .then_inc(e_xe, 1)
                if is_live(u, N):
                    gelu(1)
                if is_live(b, N):
                    wait(act, e_O, b - 7)
                    for c in range(C):
                        act.wait_ge(e_PT, C * b + c + 1)
                        copy(E_PT[(r - 1) % 8][:, c].rearrange("p n k -> p (n k)"), bank[1 + c][0:KB, 0:NB * P])\
                            .then_inc(e_PTe, 1)
            walk(act, N, LEADE, UE, TAILE, phase_e)

        @block.vector
        def _(dve):
            v = nc.vector

            dve.wait_ge(w_prep, 16 * 10)
            dve.wait_ge(c_set, 3)
            v.tensor_copy(bvwide, bvcol.unsqueeze(2).broadcast_to([D, H, P])).then_inc(p_cp, 1)
            dve.wait_ge(p_mm, 1)
            v.tensor_copy(wvT, bank[0][:, 0:H * D].rearrange("p (h d) -> p h d", h=H)).then_inc(p_cp, 1)
            dve.wait_ge(p_mm, 2)
            for c in range(C):
                v.tensor_copy(gamT[:, c, :], bank[2][:, 0:E])
            v.tensor_copy(insmean, bank[1][:, 0:1]).then_inc(p_cp, 1)
            dve.wait_ge(p_cp, 3)
            v.tensor_copy(inswide, insmean.broadcast_to([D, D]))
            CE = C * E
            v.tensor_copy(inssel[:, 0:(CE - 1) * (CE + 1) + 1:CE + 1], insmean.broadcast_to([D, CE])).then_inc(p_cp, 1)
            dve.wait_ge(p_mm, 3)
            dve.wait_ge(c_set, 4)
            v.tensor_tensor(crow[:, :], bank[3][0:P, 0:D], b1row, ALU.add).then_inc(p_cp, 1)
            v.tensor_copy(wvo[:, :, :].rearrange("p h d -> p (h d)"), bank[4][:, 0:H * D]).then_inc(p_cp, 1)
            dve.wait_ge(p_mm, 4)
            v.tensor_copy(rgrow[:, :], bank[5][0:P, 0:E])
            v.tensor_copy(gamcol, bank[5][0:CE, 16:17]).then_inc(p_cp, 1)
            v.tensor_copy(gamrow, bank[6][:, 0:E]).then_inc(p_cp, 1)
            dve.wait_ge(p_cp, 8)
            v.tensor_tensor(wx[:, :, :], wx[:, :, :], gamrow.unsqueeze(2).broadcast_to([D, E, D]), ALU.mult)\
                .then_inc(p_cp, 1)
            dve.wait_ge(w_eb, 32)
            v.scalar_tensor_tensor(out=bmod[:, :, :].rearrange("p c d -> p (c d)"),
                                   in0=ebz.rearrange("p c d -> p (c d)"), scalar=gamcol,
                                   in1=bank[7][0:CE, 0:C * D], op0=ALU.mult, op1=ALU.add).then_inc(p_cp, 1)

            def measure(src, st, s_bn):
                for c in range(len(src)):
                    last = v.bn_stats(st[0:src[c].shape[0], c, :], src[c])
                last.then_inc(s_bn, 1)

            def condense(b, src, st, mv, s_bn, s_mv):
                wait_apart(dve, s_bn, b + 1, c_set)
                for c in range(len(src)):
                    m = src[c].shape[0]
                    last = v.bn_aggr(mv[0:m, c, :], st[0:m, c, :])
                last.then_inc(s_mv, 1)

            def normalise(b, src, dst, mv, rstd, s_rstd, s_x):
                dve.wait_ge(s_rstd, b + 1)
                for c in range(len(src)):
                    m = src[c].shape[0]
                    last = v.tensor_scalar(dst[c], src[c], mv[0:m, c, 0:1], rstd[0:m, c:c + 1],
                                           ALU.subtract, ALU.mult)
                last.then_inc(s_x, 1)

            def chunks(ap):
                return [ap[:, c, :] for c in range(C)]

            def phase_a(t, r):
                if isinstance(t, int) and t == 0:
                    dve.wait_ge(w_main, 16 * 23)
                if is_live(t, N):
                    s = r % 2
                    src = [A_xk[s]] + chunks(A_xq[s])
                    wait_apart(dve, a_in[s], dma_count(t, s, 2, 16 * (C + 1)), c_set)
                    measure(src, A_st[s], a_bn)
                b = t - 2
                if is_live(b, N):
                    s = (r - 2) % 2
                    for i in range(2):
                        dve.wait_ge(a_Q, 2 * b + i + 1)
                        wait(dve, a_S, 2 * (b - 1))
                        v.tensor_tensor(A_QT[s][:, 2 * i:2 * i + 2, :],
                                        bank[1 + i][:, 0:2 * TP].rearrange("p (h k) -> p h k", h=2),
                                        cols[:, 4 + 2 * i:6 + 2 * i].unsqueeze(2).broadcast_to([D, 2, TP]),
                                        ALU.add).then_inc(a_Qe, 1)
                if is_live(t, N):
                    condense(t, src, A_st[r % 2], A_mv[r % 2], a_bn, a_mv)
                b = t - 3
                if is_live(b, N):
                    s = (r - 3) % 2
                    score = [bank[5 + c][0:P, :].rearrange("p (h k) -> p h k", h=H) for c in range(C)]
                    for c in range(C):
                        dve.wait_ge(a_S, 2 * b + c + 1)
                        v.tensor_reduce(A_mx[s][:, c, :], score[c], AX.X, ALU.max).then_inc(a_mx, 1)
                    for c in range(C):
                        dve.wait_ge(a_mx, 2 * b + c + 1)
                        wait(dve, a_AT, 2 * b + c - 3)
                        v.tensor_tensor(A_A[s][c], score[c], A_mx[s][:, c, :].unsqueeze(2).broadcast_to([P, H, KV]),
                                        ALU.subtract).then_inc(a_sub, 1)
                if is_live(t, N):
                    s = r % 2
                    wait(dve, a_T, t - 1)
                    wait(dve, a_res, t - 1)
                    normalise(t, src, [A_xn[s][:, 0, :], A_xn[s][0:P, 1, :], A_xn[s][0:P, 2, :]],
                              A_mv[s], A_rstd[s], a_rstd, a_xn)
                b = t - 3
                if is_live(b, N):
                    for c in range(C):
                        dve.wait_ge(a_exp, 2 * b + c + 1)
                        v.tensor_reduce(A_sm[s_(r, 3)][:, c, :], A_A[s_(r, 3)][c], AX.X, ALU.add).then_inc(a_sum, 1)
                    dve.wait_ge(a_sum, 2 * b + 2)
                    wait(dve, a_An, 2 * (b - 1))
                    v.reciprocal(A_rc[s_(r, 3)], A_sm[s_(r, 3)]).then_inc(a_rcp, 1)
                b = t - 5
                if is_live(b, N):
                    dve.wait_ge(a_AV, b + 1)
                    dve.wait_ge(a_res, b + 1)
                    v.tensor_tensor(h[:, b], bank[2][0:P, 0:C * D].rearrange("p (c d) -> p c d", c=C), h[:, b],
                                    ALU.add).then_inc(a_y, 1)
                b = t - 2
                if is_live(b, N):
                    s = (r - 2) % 2
                    dve.wait_ge(a_K, b + 1)
                    wait(dve, a_S, 2 * (b - 1))
                    v.tensor_tensor(A_KT[s], bank[3][:, :].rearrange("p (h k) -> p h k", h=H),
                                    cols[:, 4 + H:4 + 2 * H].unsqueeze(2).broadcast_to([D, H, KV]),
                                    ALU.add).then_inc(a_Ke, 1)

            def s_(r, k):
                return (r - k) % 2
            walk(dve, N, LEAD, U, TAIL, phase_a)

            def phase_b(t, r):
                if isinstance(t, int) and t == 0:
                    dve.wait_ge(a_y, N)
                b = t - 4
                if is_live(b, N):
                    s = (r - 4) % 2
                    dve.wait_ge(b_x, b + 1)
                    v.tensor_tensor(h[:, b], B_h[s], B_x[s], ALU.add).then_inc(b_res, 1)
                if is_live(t, N):
                    measure(chunks(h[:, t]), B_st[r % 2], b_bn)
                if is_live(t, N):
                    wait(dve, b_ve, t - 1)
                b = t - 2
                if is_live(b, N):
                    s = (r - 2) % 2
                    dve.wait_ge(b_H, b + 1)
                    wait(dve, b_res, b - 1)
                    v.tensor_tensor(B_h[s], bank[1][0:P, 0:C * D].rearrange("p (c d) -> p c d", c=C),
                                    bfrow[:, :].unsqueeze(1).broadcast_to([P, C, D]), ALU.add).then_inc(b_h, 1)
                if is_live(t, N):
                    condense(t, chunks(h[:, t]), B_st[r % 2], B_mv[r % 2], b_bn, b_mv)
                b = t - 2
                if is_live(b, N):
                    s = (r - 2) % 2
                    wait_apart(dve, b_h, b + 1, c_set)
                    measure(chunks(B_h[s]), B_st2[s], b_bn2)
                b = t - 4
                if is_live(b, N):
                    s = (r - 4) % 2
                    dve.wait_ge(b_Q, b + 1)
                    wait(dve, b_F, b - 1)
                    v.tensor_tensor(B_q[s], bank[3][0:P, 0:C * D].rearrange("p (c d) -> p c d", c=C),
                                    barow[:, :].unsqueeze(1).broadcast_to([P, C, D]), ALU.add).then_inc(b_q, 1)
                b = t - 2
                if is_live(b, N):
                    s = (r - 2) % 2
                    condense(b, chunks(B_h[s]), B_st2[s], B_mv2[s], b_bn2, b_mv2)
                b = t - 3
                if is_live(b, N):
                    s = (r - 3) % 2
                    wait(dve, b_T2, b - 1)
                    wait(dve, b_res, b - 1)
                    normalise(b, chunks(B_h[s]), chunks(B_x[s]), B_mv2[s], B_rstd2[s], b_rstd2, b_x)
            walk(dve, N, LEAD, U, TAIL, phase_b)

            ND = NF - 1
            dve.wait_ge(k_mm, 1)
            dve.wait_ge(b_P, N)
            v.memset(K_sel, LOWEST)
            v.memset(K_cr, LOWEST)
            v.memset(K_w, 1.0 / DELAYS).then_inc(k_cp, 1)
            dve.wait_ge(k_cp, 1)
            v.tensor_copy(K_cr[:, 0:ND], bank[5][0:N, 1:NF]).then_inc(k_cp, 1)
            dve.wait_ge(k_cp, 2)
            v.max(K_m8, K_cr).then_inc(k_cp, 1)
            dve.wait_ge(k_cp, 3)
            v.tensor_copy(K_sel[:, 0:PAIRS], K_m8[:, 0:PAIRS]).then_inc(k_cp, 1)
            dve.wait_ge(k_cp, 4)
            v.match_replace(K_mr, K_sel, K_cr, TAKEN).then_inc(k_own, 1)
            dve.wait_ge(k_own, 1)
            v.tensor_scalar(K_w[:, 1:NF], K_mr[:, 0:ND], TAKEN, 2.0 / DELAYS, ALU.is_equal, ALU.mult).then_inc(k_cp, 1)
            dve.wait_ge(k_mm, 2)
            v.tensor_copy(K_wT, bank[6][0:NF, 0:N]).then_inc(k_cp, 1)
            dve.wait_ge(k_mm, 3)
            v.tensor_copy(wfreq[:, :], bank[7][0:NF, 0:N]).then_inc(k_cp, 1)

            for s in range(2):
                v.memset(C_lg[s], LOWEST)
                v.memset(C_sel[s], LOWEST).then_inc(c_set2, 1)
            dve.wait_ge(c_set2, 2)
            dve.wait_ge(b_res, N)

            def phase_c(t, r):
                b = t - 4
                if is_live(b, N):
                    s = (r - 4) % 2
                    dve.wait_ge(c_exp, b + 1)
                    v.tensor_reduce(C_sm[s], C_ex[s], AX.X, ALU.add).then_inc(c_sum, 1)
                b = t - 5
                if is_live(b, N):
                    acc = C_h[(r - 5) % 4]
                    dve.wait_ge(c_B, b + 1)
                    dve.wait_ge(c_stt, E * (b + 1))
                    v.tensor_tensor(acc, bank[7][0:P, 128:128 + C * D].rearrange("p (c d) -> p c d", c=C), acc,
                                    ALU.add).then_inc(c_hb, 1)
                b = t - 4
                if is_live(b, N):
                    s = (r - 4) % 2
                    dve.wait_ge(c_sum, b + 1)
                    v.reciprocal(C_rc[s], C_sm[s])
                    dve.wait_ge(c_mr, b + 1)
                    v.scalar_tensor_tensor(out=C_ex[s], in0=C_mr[s][:, :, 0:E], scalar=TAKEN, in1=C_ex[s],
                                           op0=ALU.is_equal, op1=ALU.mult).then_inc(c_cu, 1)
                b = t - 4
                if is_live(b, N):
                    s = (r - 4) % 2
                    dve.wait_ge(c_cu, b + 1)
                    v.tensor_tensor(C_c[s], C_ex[s], C_rc[s].unsqueeze(2).broadcast_to([P, C, E]), ALU.mult)\
                        .then_inc(c_c, 1)
                b = t - 5
                if is_live(b, N):
                    dve.wait_ge(c_add2, b + 1)
                    dve.wait_ge(c_hb, b + 1)
                    v.tensor_tensor(h[:, b], C_h[(r - 5) % 4], C_u[:, :, 0, :], ALU.add).then_inc(c_out, 1)
                if is_live(t - 1, N):
                    wait(dve, c_ve, t - 2)
                b = t - 3
                if is_live(b, N):
                    s = (r - 3) % 2
                    dve.wait_ge(c_L, b + 1)
                    v.tensor_tensor(C_lg[s][:, :, 0:E], bank[2][0:P, 0:C * E].rearrange("p (c e) -> p c e", c=C),
                                    rgrow[:, :].unsqueeze(1).broadcast_to([P, C, E]), ALU.add).then_inc(c_lg, 1)
                b = t - 1
                if is_live(b, N):
                    dve.wait_ge(c_I, b + 1)
                    wait(dve, c_out, b - 3)
                    v.tensor_tensor(C_h[(r - 1) % 4], bank[0][0:P, 0:C * D].rearrange("p (c d) -> p c d", c=C),
                                    h[:, b], ALU.add).then_inc(c_h, 1)
                b = t - 3
                if is_live(b, N):
                    s = (r - 3) % 2
                    wait_apart(dve, c_lg, b + 1, c_set)
                    for c in range(C):
                        last = v.max(C_m8[s][:, c, :], C_lg[s][:, c, 0:E])
                    last.then_inc(c_m8, 1)
                b = t - 1
                if is_live(b, N):
                    wait_apart(dve, c_h, b + 1, c_set)
                    measure(chunks(C_h[(r - 1) % 4]), C_st[(r - 1) % 2], c_bn)
                b = t - 3
                if is_live(b, N):
                    s = (r - 3) % 2
                    dve.wait_ge(c_m8, b + 1)
                    v.tensor_tensor(C_ex[s], C_lg[s][:, :, 0:E], C_m8[s][:, :, 0:1].broadcast_to([P, C, E]),
                                    ALU.subtract).then_inc(c_sub, 1)
                    v.tensor_copy(C_sel[s][:, :, 0:2], C_m8[s][:, :, 0:2]).then_inc(c_sel, 1)
                b = t - 1
                if is_live(b, N):
                    s = (r - 1) % 2
                    condense(b, chunks(C_h[(r - 1) % 4]), C_st[s], C_mv[s], c_bn, c_mv)
                b = t - 4
                if is_live(b, N):
                    s = (r - 4) % 2
                    acc = C_h[(r - 4) % 4]
                    dve.wait_ge(c_c, b + 1)
                    for e in range(1):
                        for c in range(C):
                            dve.wait_ge(c_E, 4 * b + c + 1)
                            v.scalar_tensor_tensor(out=acc[:, c, :], in0=bank[3 + 2 * c][0:P, e * D:(e + 1) * D],
                                                   scalar=C_c[s][:, c, e:e + 1], in1=acc[:, c, :],
                                                   op0=ALU.mult, op1=ALU.add).then_inc(c_stt, 1)
                b = t - 3
                if is_live(b, N):
                    s = (r - 3) % 2
                    wait_apart(dve, c_sel, b + 1, c_set)
                    for c in range(C):
                        last = v.match_replace(C_mr[s][:, c, :], C_sel[s][:, c, :], C_lg[s][:, c, :], TAKEN)
                    last.then_inc(c_mr, 1)
                b = t - 4
                if is_live(b, N):
                    s = (r - 4) % 2
                    acc = C_h[(r - 4) % 4]
                    for e in range(1, E // 2):
                        for c in range(C):
                            dve.wait_ge(c_stt, E * b + 2 * e + c - 1)
                            v.scalar_tensor_tensor(out=acc[:, c, :], in0=bank[3 + 2 * c][0:P, e * D:(e + 1) * D],
                                                   scalar=C_c[s][:, c, e:e + 1], in1=acc[:, c, :],
                                                   op0=ALU.mult, op1=ALU.add).then_inc(c_stt, 1)
            walk(dve, N, LEAD, U, TAIL, phase_c)

            dve.wait_ge(c_out, N)
            for s in range(4):
                last = v.memset(D_x[s][:, :, D:D + 1], 1.0)
            last.then_inc(c_set2, 1)
            dve.wait_ge(c_set2, 3)

            def phase_d(t, r):
                o = bank[2][0:P, 0:C * (D + 1)].rearrange("p (c d) -> p c d", c=C)
                lg = bank[4][0:P, 0:C * E].rearrange("p (c e) -> p c e", c=C)
                if is_live(t, N):
                    measure(chunks(h[:, t]), D_st[r % 2], d_bn)
                b = t - 6
                if is_live(b, N):
                    s = (r - 6) % 2
                    dve.wait_ge(d_L, b + 1)
                    v.tensor_reduce(D_mx[s], lg, AX.X, ALU.max).then_inc(d_mx, 1)
                if is_live(t, N):
                    wait(dve, d_ve, t - 1)
                b = t - 3
                if is_live(b, N):
                    s = (r - 3) % 2
                    dve.wait_ge(d_O, b + 1)
                    v.reciprocal(D_rc[s], o[:, :, D]).then_inc(d_rcp, 1)
                b = t - 6
                if is_live(b, N):
                    s = (r - 6) % 2
                    dve.wait_ge(d_mx, b + 1)
                    v.tensor_tensor(D_lg[s], lg, D_mx[s].unsqueeze(2).broadcast_to([P, C, E]),
                                    ALU.subtract).then_inc(d_sub, 1)
                if is_live(t, N):
                    condense(t, chunks(h[:, t]), D_st[r % 2], D_mv[r % 2], d_bn, d_mv)
                b = t - 3
                if is_live(b, N):
                    dve.wait_ge(d_rcp, b + 1)
                    s = (r - 3) % 2
                    for c in range(C):
                        last = v.scalar_tensor_tensor(out=h[:, b, c, :], in0=o[:, c, 0:D], scalar=D_rc[s][:, c:c + 1],
                                                      in1=h[:, b, c, :], op0=ALU.mult, op1=ALU.add)
                    last.then_inc(d_h, 1)
                b = t - 4
                if is_live(b, N):
                    s = (r - 4) % 2
                    wait(dve, d_T2, b - 1)
                    normalise(b, chunks(h[:, b]), chunks(D_x2[s]), D_mv2[s], D_rstd2[s], d_rstd2, d_x2)
                b = t - 3
                if is_live(b, N):
                    s = (r - 3) % 2
                    wait_apart(dve, d_h, b + 1, c_set)
                    measure(chunks(h[:, b]), D_st2[s], d_bn2)
                b = t - 6
                if is_live(b, N):
                    s = (r - 6) % 2
                    dve.wait_ge(d_exp, b + 1)
                    v.tensor_reduce(D_sm[s], D_lg[s], AX.X, ALU.add).then_inc(d_sum, 1)
                b = t - 3
                if is_live(b, N):
                    s = (r - 3) % 2
                    condense(b, chunks(h[:, b]), D_st2[s], D_mv2[s], d_bn2, d_mv2)
                b = t - 6
                if is_live(b, N):
                    s = (r - 6) % 2
                    dve.wait_ge(d_sum, b + 1)
                    v.reciprocal(D_rc2[s], D_sm[s]).then_inc(d_rcp2, 1)
                b = t - 6
                if is_live(b, N):
                    s = (r - 6) % 2
                    dve.wait_ge(d_rcp2, b + 1)
                    dst = gates[:, :, E * b:E * b + E] if isinstance(b, int) else gates[:, :, bass.ds(b * E, E)]
                    v.tensor_tensor(dst, D_lg[s], D_rc2[s].unsqueeze(2).broadcast_to([P, C, E]), ALU.mult)\
                        .then_inc(d_S, 1)
            walk(dve, N, LEAD, U, TAIL, phase_d)

            dve.wait_ge(d_S, N)
            dve.wait_ge(d_T2, N)
            v.memset(T_one, 1.0)
            for s in range(2):
                v.memset(T_id[s], -1.0)
                v.memset(T_s[s], LOWEST).then_inc(t_set, 1)
            dve.wait_ge(t_set, 2)

            def slots_out(g):
                n = min(GB, N - g * GB) * E
                dve.wait_ge(t_mm2, g + 1)
                v.tensor_copy(slots[:, :, g * 128:g * 128 + n],
                              bank[2 + g % 2][0:P, 0:C * 128].rearrange("p (c k) -> p c k", c=C)[:, :, 0:n])\
                    .then_inc(t_slot, 1)
            rounds = (K + 7) // 8
            short = K - 8 * (rounds - 1)
            assert 8 - short <= 3
            done = [0, 0]
            for first in range(0, NG, 2):
                pair = [(g, g % 2, min(GB, N - g * GB) * E) for g in range(first, min(first + 2, NG))]
                for g, s, n in pair:
                    dve.wait_ge(t_mm, g + 1)
                    v.tensor_copy(T_s[s][0:n, 0:T], bank[g % 2][0:n, 0:T]).then_inc(t_cp, 1)
                for k in range(rounds):
                    for g, s, n in pair:
                        if k == 0:
                            dve.wait_ge(t_cp, g + 1)
                        else:
                            dve.wait_ge(t_own[s], done[s])
                        src = T_s[s] if k == 0 else T_w[s]
                        v.max(T_m8[s][0:n], src[0:n, 0:T]).then_inc(t_own[s], 1)
                        done[s] += 1
                    if k == rounds - 1 and short < 8:
                        for g, s, n in pair:
                            dve.wait_ge(t_own[s], done[s])
                            v.memset(T_m8[s][0:n, short:], LOWEST).then_inc(t_own[s], 1)
                            done[s] += 1
                    for g, s, n in pair:
                        src = T_s[s] if k == 0 else T_w[s]
                        dve.wait_ge(t_own[s], done[s])
                        v.match_replace(T_w[s][0:n], T_m8[s][0:n], src[0:n], CHOSEN).then_inc(t_own[s], 1)
                        done[s] += 1
                    if k == 0:
                        for g in range(max(first - 2, 0), first):
                            slots_out(g)
                for g, s, n in pair:
                    dve.wait_ge(t_own[s], done[s])
                    v.tensor_scalar(T_w[s][0:n, 0:T], T_w[s][0:n, 0:T], CHOSEN, None, ALU.is_equal)\
                        .then_inc(t_own[s], 1)
                    done[s] += 1
                for g, s, n in pair:
                    dve.wait_ge(t_own[s], done[s])
                    v.tensor_tensor_scan(T_pos[s][0:n], T_one[0:n], T_w[s][0:n, 0:T], 0.0, ALU.mult, ALU.add)\
                        .then_inc(t_own[s], 1)
                    done[s] += 1
                for g, s, n in pair:
                    dve.wait_ge(t_own[s], done[s])
                    v.tensor_tensor(T_pos[s][0:n], T_pos[s][0:n], T_w[s][0:n, 0:T], ALU.mult).then_inc(t_own[s], 1)
                    done[s] += 1
                for g, s, n in pair:
                    dve.wait_ge(t_own[s], done[s])
                    wait(dve, t_mm2, g - 1)
                    v.tensor_scalar(T_id[s][0:n, 0:T], T_pos[s][0:n], -1.0, None, ALU.add).then_inc(t_id, 1)
            for g in range(max(NG - 2, 0) // 2 * 2, NG):
                slots_out(g)

            def phase_e(t, r):
                b = t - 1
                if is_live(b, N):
                    dve.wait_ge(e_xh, b + 1)
                    v.tensor_tensor(E_xl[(r - 1) % 2][:, :, :], E_x[(r - 1) % 2], E_xh[(r - 1) % 2][:, :, :],
                                    ALU.subtract).then_inc(e_xl, 1)
                if is_live(t, N):
                    s = r % 2
                    if isinstance(t, int) and t == 0:
                        dve.wait_ge(t_slot, NG)
                    measure(chunks(h[:, t]), E_st[s], e_bn)
                b = t - 9
                if is_live(b, N):
                    dve.wait_ge(e_VT, b + 1)
                    wait(dve, e_O, b)
                    v.tensor_copy(E_v.rearrange("p n d -> p (n d)"), bank[6][0:KB, 0:NB * D]).then_inc(e_vt, 1)
                if is_live(t, N):
                    s = r % 2
                    condense(t, chunks(h[:, t]), E_st[s], E_mv[s], e_bn, e_mv)
                    for c in range(C):
                        wait(dve, e_X, t - 1)
                        wait(dve, e_PG, C * (t - 1))
                        no = slots[:, c, E * t:E * t + E] if isinstance(t, int) else slots[:, c, bass.ds(t * E, E)]
                        v.tensor_tensor(E_P[s][:, c, :, :], slotno[:, :].unsqueeze(1).broadcast_to([P, E, K]),
                                        no.unsqueeze(2).broadcast_to([P, E, K]), ALU.is_equal).then_inc(e_P, 1)
                    normalise(t, chunks(h[:, t]), chunks(E_x[s]), E_mv[s], E_rstd[s], e_rstd, e_x)
                u = t - 5
                e0 = 2 * ((r - 5) % 4)
                qs = ((r - 5) % 8) // 4

                def down(k):
                    dve.wait_ge(e_V, u * 2 + k + 1)
                    if (r - 5) % 4 == 0 and k == 0:
                        wait(dve, e_VT, u - 4)
                    v.tensor_scalar(E_vt[qs][:, :, e0 + k, :], bank[5][:, 0:Q4 * K].rearrange("p (b k) -> p b k", b=Q4),
                                    b2col[:, e0 + k:e0 + k + 1], None, ALU.add).then_inc(e_v, 1)

                if is_live(u, N):
                    down(0)
                b = t - 9
                if is_live(b, N):
                    dve.wait_ge(e_O, b + 1)
                    v.tensor_tensor(h[:, b], bank[7][0:P, 0:C * D].rearrange("p (c d) -> p c d", c=C), h[:, b],
                                    ALU.add).then_inc(e_o, 1)
                if is_live(u, N):
                    down(1)
            walk(dve, N, LEADE, UE, TAILE, phase_e)


_INS = ['L0_tok_g1', 'L0_tok_b1', 'L0_tok_Wq', 'L0_tok_bq', 'L0_tok_Wk', 'L0_tok_bk', 'L0_tok_Wv', 'L0_tok_bv',
        'L0_tok_Wo', 'L0_tok_bo', 'L0_tok_g2', 'L0_tok_b2', 'L0_tok_Wf', 'L0_tok_bf', 'L0_attn_W', 'L0_attn_b',
        'L0_ffn_Ins_tk', 'L0_ffn_gate_w', 'L0_ffn_expert_w', 'L0_ffn_expert_b', 'L0_ffn_gamma_w', 'L0_ffn_beta_w',
        'L0_ffn_rmod_w', 'L1_ffn_Wg', 'L1_ffn_W1', 'L1_ffn_b1', 'L1_ffn_W2', 'L1_ffn_b2']


def _fourier_tables(T):
    import numpy as np
    half = T // 2 + 1
    angle = 2.0 * np.pi * (np.outer(np.arange(T), np.arange(half)) % T) / T
    weight = np.full(half, 2.0 / T)
    weight[0] = 1.0 / T
    forward, inverse = [], []
    for f in (np.cos, np.sin):
        table = np.zeros((2 * half, half))
        table[:T] = f(angle)
        forward.append(table.astype(np.float32))
        inverse.append(np.ascontiguousarray((table * weight).T.astype(np.float32)))
    return forward + inverse


def kernel(**inputs):
    import numpy as _np
    import concourse.bacc as _bacc
    from concourse import mybir as _mybir
    from concourse.bass_utils import run_bass_kernel_spmd as _run

    nc = _bacc.Bacc("TRN2", target_bir_lowering=False, num_devices=1)
    x = _np.ascontiguousarray(inputs["x"])
    arrays, args = {}, []

    def give(name, a):
        arrays[name] = a
        args.append(nc.dram_tensor(name, a.shape, _mybir.dt.from_np(a.dtype), kind="ExternalInput").ap())

    n, s, d = x.shape
    t = s - 128
    give("in_x_dram", x)
    for name, table in zip(("fwd_cos", "fwd_sin", "inv_cos", "inv_sin"), _fourier_tables(t)):
        give(f"table_{name}_dram", table)
    for name in _INS:
        give(f"in_{name}_dram", _np.ascontiguousarray(inputs[name]))
    result = nc.dram_tensor("out_0_dram", (n, t, d), _mybir.dt.float32, kind="ExternalOutput").ap()
    audio_tower(nc, *args, result)
    r = _run(nc, [arrays], core_ids=[0])
    return r.results[0]["out_0_dram"]
```
